# Optimizing a Trainium2 kernel written in Bass

```python
import numpy as np
import jax
import jax.numpy as jnp

def _softmax(x, axis=-1):
    return jax.nn.softmax(x, axis=axis)

def _gelu(x):
    return jax.nn.gelu(x, approximate=True)

def _silu(x):
    return jax.nn.silu(x)

def _sigmoid(x):
    return jax.nn.sigmoid(x)

def _layernorm(x, axis=-1, eps=1e-05):
    m = jnp.mean(x, axis=axis, keepdims=True)
    v = jnp.var(x, axis=axis, keepdims=True)
    return (x - m) / jnp.sqrt(v + eps)

def _scatter_add(tgt, idx, src, axis=0):
    return tgt.at[idx].add(src)

def _segment_sum(src, seg, n):
    return jax.ops.segment_sum(src, seg, n)
kernel_name = 'mk_cond_resid_d2_seqx_r2_d67c12'

def setup_inputs(seed: int=0):
    np.random.seed(seed)
    _w = jnp.asarray

    def _rec_inputs():
        import jax
        import jax.numpy as jnp
        _rk = jax.random.key(seed)
        x = -0.000125 + 0.9999 * jax.random.normal(jax.random.fold_in(_rk, 1), (2, 2048, 512), jnp.float32)
        _lenS = 2048 - jax.random.randint(jax.random.fold_in(_rk, 7), (2,), 0, max(1, 2048 // 4) + 1, jnp.int32)
        _lenS2 = 2048 - jax.random.randint(jax.random.fold_in(_rk, 8), (2,), 0, max(1, 2048 // 4) + 1, jnp.int32)
        cond_1024 = -0.00493535 + 1.00056 * jax.random.normal(jax.random.fold_in(_rk, 11), (2, 512), jnp.float32)
        return (x, cond_1024)
    x, cond_1024 = _rec_inputs()

    def _L0_cond_setup():
        import jax, jax.numpy as jnp
        import numpy as np
        N, T, D, H = (64, 256, 512, 512)
        key = jax.random.key(seed)
        k1, k2, k3, k4 = jax.random.split(key, 4)
        x = jax.random.normal(k1, (N, T, D), dtype=jnp.float32)
        h0 = jax.random.normal(k2, (N, H), dtype=jnp.float32)
        Wx = jax.random.normal(k3, (D, H), dtype=jnp.float32) / jnp.sqrt(jnp.float32(D))
        Wh = jax.random.normal(k4, (H, H), dtype=jnp.float32) / jnp.sqrt(jnp.float32(H))
        b = jnp.zeros((H,), dtype=jnp.float32)
        return {'x': x, 'h0': h0, 'Wx': Wx, 'Wh': Wh, 'b': b}
    _L0_cond_all = _L0_cond_setup()
    _L0_cond_in = {k: v for k, v in _L0_cond_all.items() if k in ('Wx', 'Wh', 'b')}
    del _L0_cond_all

    def _L1_cond_setup():
        import jax, jax.numpy as jnp
        import numpy as np
        D, HS, HE, E, K = (512, 1024, 512, 8, 2)
        B, T = (4, 512)
        N_SHARED = 1
        key = jax.random.key(seed)
        ks = jax.random.split(key, 9)
        g = lambda k, shape, s: jax.random.normal(k, shape, jnp.float32) * s
        return {'x': g(ks[0], (B, T, D), 1.0), 't_emb': g(ks[1], (B, D), 1.0), 'router_W': g(ks[2], (2 * D, E), 0.01), 'router_bias': jnp.zeros((E,), jnp.float32), 'w1': g(ks[3], (D, HS), 0.02), 'w3': g(ks[4], (D, HS), 0.02), 'w2': g(ks[5], (HS, D), 0.02), 'W1e': g(ks[6], (E, D, HE), 0.02), 'W2e': g(ks[7], (E, HE, D), 0.02)}
    _L1_cond_all = _L1_cond_setup()
    _L1_cond_in = {k: v for k, v in _L1_cond_all.items() if k in ('router_W', 'router_bias', 'w1', 'w3', 'w2', 'W1e', 'W2e')}
    del _L1_cond_all
    return {'x': x, 'cond_1024': cond_1024, 'L0_cond_Wx': _L0_cond_in['Wx'], 'L0_cond_Wh': _L0_cond_in['Wh'], 'L0_cond_b': _L0_cond_in['b'], 'L1_cond_router_W': _L1_cond_in['router_W'], 'L1_cond_router_bias': _L1_cond_in['router_bias'], 'L1_cond_w1': _L1_cond_in['w1'], 'L1_cond_w3': _L1_cond_in['w3'], 'L1_cond_w2': _L1_cond_in['w2'], 'L1_cond_W1e': _L1_cond_in['W1e'], 'L1_cond_W2e': _L1_cond_in['W2e']}

def reference(x, cond_1024, L0_cond_Wx, L0_cond_Wh, L0_cond_b, L1_cond_router_W, L1_cond_router_bias, L1_cond_w1, L1_cond_w3, L1_cond_w2, L1_cond_W1e, L1_cond_W2e):
    import jax
    import jax.numpy as jnp

    def _L0_cond_ref(x, h0, Wx, Wh, b):
        import jax, jax.numpy as jnp
        import numpy as np
        N, T, D, H = (64, 256, 512, 512)
        xw = jnp.einsum('ntd,dh->nth', x, Wx) + b

        def step(prev_h, xw_t):
            next_h = jnp.tanh(xw_t + prev_h @ Wh)
            return (next_h, next_h)
        _, hs = jax.lax.scan(step, h0, jnp.swapaxes(xw, 0, 1))
        return jnp.swapaxes(hs, 0, 1)

    def _L1_cond_ref(x, t_emb, router_W, router_bias, w1, w3, w2, W1e, W2e):
        import jax, jax.numpy as jnp
        import numpy as np
        D, HS, HE, E, K = (512, 1024, 512, 8, 2)
        B, T = (4, 512)
        N_SHARED = 1
        Bb, Tt, C = x.shape
        xf = x.reshape(-1, C)
        tf = jnp.broadcast_to(t_emb[:, None, :], (Bb, Tt, C)).reshape(-1, C)
        N = xf.shape[0]
        shared = jax.nn.silu(xf @ w1) * (xf @ w3) @ w2
        s = jax.nn.sigmoid((jnp.concatenate([xf, tf], axis=-1) @ router_W).astype(jnp.float32))
        sel_scores = s + router_bias
        _, topk_idx = jax.lax.top_k(sel_scores, K)
        s_sel = jnp.take_along_axis(s, topk_idx, axis=1)
        denom = s_sel.sum(axis=1, keepdims=True)
        gates = jnp.where(denom > 1e-09, s_sel / (denom + 1e-09), 1.0 / K).astype(x.dtype)
        combine = jnp.zeros((N, E), x.dtype).at[jnp.arange(N)[:, None], topk_idx].add(gates)
        h = jax.nn.gelu(jnp.einsum('nc,ech->enh', xf, W1e), approximate=False)
        y = jnp.einsum('enh,ehc->enc', h, W2e)
        routed = jnp.einsum('ne,enc->nc', combine, y)
        return ((shared + routed) / (N_SHARED + K)).reshape(Bb, Tt, C)
    x = x + _L0_cond_ref(x, cond_1024, L0_cond_Wx, L0_cond_Wh, L0_cond_b)
    x = x + _L1_cond_ref(x, cond_1024, L1_cond_router_W, L1_cond_router_bias, L1_cond_w1, L1_cond_w3, L1_cond_w2, L1_cond_W1e, L1_cond_W2e)
    return x

_drawn_inputs = setup_inputs


def setup_inputs(seed=0):
    import zlib

    import numpy as np

    out = dict(_drawn_inputs(seed))
    spreads = {'L0_cond_b': (0.0, 0.1), 'L1_cond_router_bias': (0.0, 1.012)}
    factors = {'cond_1024': 2.714, 'L1_cond_router_W': 9.802}
    for name, (base, spread) in spreads.items():
        noise = np.random.default_rng([zlib.crc32(name.encode()), seed]).standard_normal(out[name].shape)
        drawn = base * np.exp(spread * noise) if base else spread * noise
        out[name] = jnp.asarray(drawn.astype(out[name].dtype))
    for name, factor in factors.items():
        out[name] = (out[name] * factor).astype(out[name].dtype)
    return out
```

```python
import math

import concourse.bass as bass
from concourse import mybir
from contextlib import ExitStack


def rnn_then_moe_kernel(
    nc: bass.Bass,
    x: bass.AP,
    cond: bass.AP,
    Wx: bass.AP,
    Wh: bass.AP,
    b_rnn: bass.AP,
    router_W: bass.AP,
    router_bias: bass.AP,
    w1: bass.AP,
    w3: bass.AP,
    w2: bass.AP,
    W1e: bass.AP,
    W2e: bass.AP,
    out: bass.AP,
):
    f32 = mybir.dt.float32
    f16 = mybir.dt.float16
    ALU = mybir.AluOpType
    ACT = mybir.ActivationFunctionType
    AX = mybir.AxisListType
    ds = bass.ds

    P = 128
    B, T, C = x.shape
    E, _, HE = W1e.shape
    HS = w1.shape[1]
    TB = P
    NB = T // TB
    KC = C // P
    N = B * TB
    HALVES = HS // HE
    JC = HE // P
    UNITS = HALVES + E
    CH = UNITS * JC
    PART = KC * C
    WS = 64.0
    GS = 2.0 * WS
    OS = 1.0 / (3.0 * GS * WS)
    HSTEPS = 16
    ESTEPS = (TB - HALVES * HSTEPS) // E
    UP_H = 12
    UP_E = ESTEPS // 2
    SL = 4
    NSH = 3 * HALVES
    NEX = 2 * E
    BIG = 1.0e30

    sc13 = nc.dram_tensor("shared_up_parts", [HALVES * JC, P, 2, 2, KC, P], f16).ap()
    sc2 = nc.dram_tensor("shared_down_parts", [HALVES, P, 2 * PART], f16).ap()

    ctx = ExitStack()
    with ctx:
        def sb(name, shape, dt):
            return ctx.enter_context(nc.sbuf_tensor(name, shape, dt))

        def sem(name):
            return ctx.enter_context(nc.semaphore(name))

        wx = sb("wx", [P, 2 * PART], f16)
        wh = sb("wh", [P, 2 * PART], f16)
        we1 = sb("we1", [P, E * 2 * PART], f16)
        we2 = sb("we2", [P, E * 2 * PART], f16)
        stream = sb("stream", [P, 2 * PART], f32)
        s13 = stream[:, 0:PART].bitcast(f16).rearrange("p (s w q k c) -> p s w q k c", s=2, w=2, q=2, k=KC)
        s2 = stream[:, PART:2 * PART].bitcast(f16)
        stage = stream[:, :].rearrange("p (s n) -> p s n", s=2)
        hp = sb("hp", [P, KC, 2, B, 1], f16)
        hist = sb("hist", [P, KC, B, TB], f32)
        xw = sb("xw", [P, KC, B, TB + 2], f32)
        pre = sb("pre", [P, KC, B, 1], f32)
        xn = sb("xn", [P, B, C], f32)
        xt = sb("xt", [P, KC, N], f32)
        xp = sb("xp", [P, 2, KC, N], f16)
        x1 = sb("x1", [P, KC, N], f32)
        x1p = sb("x1p", [P, 2, KC, N], f16)
        et = sb("et", [P, 2, N], f32)
        ut = sb("ut", [P, N], f32)
        gt = sb("gt", [P, 2, N], f32)
        hid = sb("hid", [P, JC, 2, N], f16)
        acc = sb("acc", [P, B, C], f32)
        ident = sb("ident", [P, P], f32)
        ones = sb("ones", [1, P], f32)
        ct = sb("ct", [P, KC, B, 1], f32)
        b64 = sb("b64", [P, KC], f32)
        rw = sb("rw", [P, 2 * KC, E], f32)
        rb = sb("rb", [P, B, E], f32)
        rev = sb("rev", [P, B, E], f32)
        trow = sb("trow", [1, B * E], f32)
        base = sb("base", [P, B * E], f32)
        nlog = sb("nlog", [P, B * E], f32)
        pw = sb("pw", [P, B * E], f32)
        sg = sb("sg", [P, B, E], f32)
        sel = sb("sel", [P, B, E], f32)
        m1 = sb("m1", [P, B, E], f32)
        oh1 = sb("oh1", [P, B, E], f32)
        oh2 = sb("oh2", [P, B, E], f32)
        mx = sb("mx", [P, B, 1], f32)
        den = sb("den", [P, B, 1], f32)
        okd = sb("okd", [P, B, 1], f32)
        alt = sb("alt", [P, B, 1], f32)
        gates = sb("gates", [P, B * E], f32)

        def bank(name):
            return ctx.enter_context(nc.psum_tensor(name, [P, 512], f32))

        zb = [bank(f"zb{i}") for i in range(2)]
        ub = [bank(f"ub{i}") for i in range(4)]
        db = [bank(f"db{i}") for i in range(2)]
        rbk = ub[3]
        z = [zb[i][:, 0:KC * 3 * B].rearrange("p (j c b) -> p j c b", j=KC, c=3) for i in range(2)]

        small_in = sem("small_in")
        x_in = sem("x_in")
        wxh_in = sem("wxh_in")
        staged = [sem("staged0"), sem("staged1")]
        s13_in = [sem("s13_in0"), sem("s13_in1")]
        s2_in = sem("s2_in")
        scratch_out = sem("scratch_out")
        acc_free = sem("acc_free")
        consts = sem("consts")
        ident0 = sem("ident0")
        b_scaled = sem("b_scaled")
        h0_hi = sem("h0_hi")
        t_ps = sem("t_ps")
        t_row = sem("t_row")
        w_hi = sem("w_hi")
        w_split = sem("w_split")
        z_ready = sem("z_ready")
        seeded = sem("seeded")
        pre_ready = sem("pre_ready")
        h_kept = sem("h_kept")
        h_hi = sem("h_hi")
        h_ready = sem("h_ready")
        xt_ps = sem("xt_ps")
        xt_ready = sem("xt_ready")
        xp_hi = sem("xp_hi")
        xp_ready = sem("xp_ready")
        xw_ps = sem("xw_ps")
        xw_ready = sem("xw_ready")
        x1_ready = sem("x1_ready")
        x1_hi = sem("x1_hi")
        x1p_ready = sem("x1p_ready")
        x1_rows = sem("x1_rows")
        acc_set = sem("acc_set")
        logits = sem("logits")
        nlog_ready = sem("nlog_ready")
        pow_ready = sem("pow_ready")
        chain = sem("chain")
        up_done = sem("up_done")
        act_done = sem("act_done")
        u_done = sem("u_done")
        g_done = sem("g_done")
        hid_hi = sem("hid_hi")
        hid_ready = sem("hid_ready")
        down_done = sem("down_done")
        added = sem("added")

        block = ctx.enter_context(nc.Block())

        def chunk_no(m, w, j):
            return m * CH + w * JC + j

        def unit_no(m, w):
            return m * UNITS + w

        XW_BANK = [2, 0, 1, 3]

        def to_scratch(sp, g):
            sp.wait_ge(w_split, 2 + SL * (g + 1))
            src = we2[:, (2 + g) * 2 * PART:(3 + g) * 2 * PART]
            if g < 2 * HALVES:
                w, h = g // HALVES, g % HALVES
                parts = src.rearrange("p (g n) -> p g n", n=C)
                for j in range(JC):
                    sp.dma_start(sc13[h * JC + j, :, w, :, :, :].rearrange("p q k c -> p (q k) c"),
                                 parts[:, :, j * P:(j + 1) * P]).then_inc(scratch_out, 16)
            else:
                sp.dma_start(sc2[g - 2 * HALVES, :, :], src).then_inc(scratch_out, 16)

        def x_block(sp, i):
            sp.wait_ge(xt_ps, i * 2)
            sp.dma_start(xn[:, :, :], x[:, ds(i * TB, TB), :].rearrange("b t c -> t b c")).then_inc(x_in, 16)

        def half_weights(sp, m, h, first=False):
            for j in range(JC):
                if j == 2 and h == 0 and not first:
                    block_out(sp, m - 1)
                if not (first and j < 2):
                    before = chunk_no(m, h, j - 2) if (h > 0 or j >= 2) else chunk_no(m - 1, HALVES - 1, JC - 2 + j)
                    sp.wait_ge(up_done, before + 1)
                sp.dma_start(s13[:, j % 2, :, :, :, :].rearrange("p w q k c -> p (w q k c)"),
                             sc13[h * JC + j, :, :, :, :, :].rearrange("p w q k c -> p (w q k c)"))\
                  .then_inc(s13_in[j % 2], 16)
            if not first:
                before = unit_no(m, h - 1) if h > 0 else unit_no(m - 1, HALVES - 1)
                sp.wait_ge(down_done, (before + 1) * B)
            sp.dma_start(s2, sc2[h, :, :]).then_inc(s2_in, 16)

        def block_out(sp, m):
            sp.wait_ge(added, (m + 1) * (UNITS * B) + 1)
            sp.dma_start(out[:, ds(m * TB, TB), :].rearrange("b t c -> t b c"), acc[:, :, :]).then_inc(acc_free, 16)

        @block.sync
        def _(sp):
            sp.dma_start(stage[:, 0, :].rearrange("p (k n) -> p k n", k=KC),
                         Wx.rearrange("(k p) n -> p k n", p=P)).then_inc(wxh_in, 16)
            sp.dma_start(stage[:, 1, :].rearrange("p (k n) -> p k n", k=KC),
                         Wh.rearrange("(k p) n -> p k n", p=P)).then_inc(wxh_in, 16)
            with nc.allow_non_contiguous_dma(reason="a few KB of constants, once"):
                sp.dma_start(b64[:, :], b_rnn.rearrange("(k p) -> p k", p=P)).then_inc(small_in, 16)
                sp.dma_start(acc[:, 0, 0:KC], b_rnn.rearrange("(k p) -> p k", p=P)).then_inc(acc_free, 16)
                for b in range(B):
                    sp.dma_start(ct[:, :, b, 0], cond[b, :].rearrange("(k p) -> p k", p=P)).then_inc(small_in, 16)
                sp.dma_start(rw[:, :, :], router_W.rearrange("(k p) e -> p k e", p=P)).then_inc(small_in, 16)
                for b in range(B):
                    sp.dma_start(rb[:, b, :], router_bias.rearrange("(o e) -> o e", o=1).to_broadcast([P, E]))\
                      .then_inc(small_in, 16)

            def k_rows(w, r0, c0):
                return w[r0:r0 + C, c0:c0 + C].rearrange("(k p) n -> p k n", p=P)

            shared = [k_rows(w, 0, h * HE) for w in (w1, w3) for h in range(HALVES)]
            shared += [k_rows(w2, h * HE, 0) for h in range(HALVES)]
            for g in range(NSH):
                sp.wait_ge(w_split, 2 + (SL * (g - 2) + SL if g >= 2 else 0))
                sp.dma_start(stage[:, g % 2, :].rearrange("p (k n) -> p k n", k=KC), shared[g])\
                  .then_inc(staged[g % 2], 16)
                if g >= 1:
                    to_scratch(sp, g - 1)
            for s, w in enumerate((W1e, W2e)):
                sp.wait_ge(w_split, 2 + SL * (NSH - 1 + s))
                if s == 1:
                    to_scratch(sp, NSH - 1)
                sp.dma_start(stage[:, s, :].rearrange("p (k n) -> p k n", k=KC),
                             w[0, :, :].rearrange("(k p) n -> p k n", p=P)).then_inc(staged[s], 16)
            with sp.Fori(1, E) as e:
                for s, w in enumerate((W1e, W2e)):
                    sp.wait_ge(w_split, e * (2 * SL) + (2 + SL * (NSH - 1 + s)))
                    sp.dma_start(stage[:, s, :].rearrange("p (k n) -> p k n", k=KC),
                                 w.rearrange("e r n -> (e r) n")[ds(e * C, C), :]
                                 .rearrange("(k p) n -> p k n", p=P)).then_inc(staged[s], 16)
            sp.wait_ge(w_split, 2 + SL * (NSH + NEX))
            sp.wait_ge(scratch_out, 16 * (2 * HALVES * JC + HALVES))
            half_weights(sp, 0, 0, first=True)
            half_weights(sp, 0, 1)
            with sp.Fori(1, NB) as i:
                half_weights(sp, i, 0)
                half_weights(sp, i, 1)
            block_out(sp, NB - 1)
            sp.wait_ge(acc_free, 16 * (NB + 1))

        def pool_pow(pool, m):
            pool.wait_ge(nlog_ready, m + 1)
            nc.gpsimd.tensor_tensor(pw[:, :], base[:, :], nlog[:, :], ALU.pow).then_inc(pow_ready, 1)

        @block.gpsimd
        def _(pool):
            nc.gpsimd.memset(ones[:, :], 1.0).then_inc(consts, 1)
            nc.gpsimd.memset(xw[:, :, :, TB:TB + 2], 0.0).then_inc(consts, 1)
            nc.gpsimd.memset(base[:, :], math.e).then_inc(consts, 1)
            for e in range(E):
                nc.gpsimd.memset(rev[:, :, e], float(E - e)).then_inc(consts, 1)
            nc.gpsimd.memset(ident[:, :], 0.0).then_inc(ident0, 1)
            pool.wait_ge(ident0, 1)
            nc.gpsimd.affine_select(out=ident[:, :], in_=ident[:, :], compare_op=ALU.not_equal, fill=1.0, base=0,
                                    pattern=[[-1, P]], channel_multiplier=1).then_inc(consts, 1)
            x_block(pool, 0)
            with pool.Fori(1, NB) as i:
                x_block(pool, i)
                pool_pow(pool, i - 1)
            pool_pow(pool, NB - 1)

        def wpart(w, q, k, c0, n):
            return w[:, q * PART + k * C + c0:q * PART + k * C + c0 + n]

        THREE = ((0, 0), (0, 1), (1, 0))

        def pe_step(pe, n, par):
            pe.wait_ge(h_hi, n + 1)
            for j in range(KC):
                for k in range(KC):
                    nc.tensor.matmul(z[par][:, j, 0, :], wpart(wh, 1, k, j * P, P), hp[:, k, 0, :, 0],
                                     start=(j == 0 and k == 0), stop=False, skip_group_check=True)
            pe.wait_ge(h_ready, n + 1)
            for j in range(KC):
                for k in range(KC):
                    last = nc.tensor.matmul(z[par][:, j, 0:2, :], wpart(wh, 0, k, j * P, P), hp[:, k, :, :, 0],
                                            start=False, stop=(k == KC - 1), skip_group_check=True)
            last.then_inc(z_ready, 1)

        def pe_inputs(pe, i):
            pe.wait_ge(x_in, (i + 1) * 16)
            for k in range(KC):
                for b in range(B):
                    o = (k % 2) * N + b * TB
                    last = nc.tensor.transpose(ub[k // 2][:, o:o + TB], xn[:, b, k * P:(k + 1) * P], ident[:, :])
                if k % 2 == 1:
                    last.then_inc(xt_ps, 1)

        def pe_xw(pe, i):
            pe.wait_ge(xp_ready, i + 1)
            for j in range(KC):
                if XW_BANK[j] < 2:
                    pe.wait_ge(xt_ready, (i + 1) * 2)
                if XW_BANK[j] == 3:
                    pe.wait_ge(nlog_ready, i)
                for k in range(KC):
                    for q, r in THREE:
                        last = nc.tensor.matmul(ub[XW_BANK[j]][:, 0:N], wpart(wx, q, k, j * P, P), xp[:, r, k, :],
                                                start=(k == 0 and q + r == 0), stop=(k == KC - 1 and q == 1))
                last.then_inc(xw_ps, 1)

        def pe_rows(pe, m):
            pe.wait_ge(x1_ready, m + 1)
            pe.wait_ge(added, m * (UNITS * B) + 1)
            for b in range(B):
                for k in range(KC):
                    last = nc.tensor.transpose(db[b][:, k * P:(k + 1) * P], x1[:, k, b * TB:(b + 1) * TB],
                                               ident[:, :])
                last.then_inc(x1_rows, 1)
            for b in range(B):
                o = rbk[:, b * E:(b + 1) * E]
                for k in range(KC):
                    nc.tensor.matmul(o, x1[:, k, b * TB:(b + 1) * TB], rw[:, k, :], start=(k == 0), stop=False)
                last = nc.tensor.matmul(o, ones[0:1, :], trow[0:1, b * E:(b + 1) * E], start=False, stop=True)
            last.then_inc(logits, 1)

        def half_ups(pe, m, h, todo):
            per = KC * len(THREE)
            for n in todo:
                j, r = divmod(n, 2 * per)
                w, r = divmod(r, per)
                k, t = divmod(r, len(THREE))
                if w == 0 and r == 0:
                    pe.wait_ge(s13_in[j % 2], (m * (HALVES * JC // 2) + (h * JC + j) // 2 + 1) * 16)
                    if j >= 2:
                        pe.wait_ge(hid_ready, chunk_no(m, h, j - 2) + 1)
                q, s = THREE[t]
                mm = nc.tensor.matmul(ub[2 * (j % 2) + w][:, 0:N], s13[:, j % 2, w, q, k, :], x1p[:, s, k, :],
                                      start=(r == 0), stop=(r == per - 1))
                if w == 1 and r == per - 1:
                    mm.then_inc(up_done, 1)

        def expert_ups(pe, e, todo):
            per = KC * len(THREE)
            for n in todo:
                j, r = divmod(n, per)
                k, t = divmod(r, len(THREE))
                q, s = THREE[t]
                mm = nc.tensor.matmul(ub[j][:, 0:N], we1[:, ds(e * (2 * PART) + (q * PART + k * C + j * P), P)],
                                      x1p[:, s, k, :], start=(r == 0), stop=(r == per - 1))
                if r == per - 1:
                    mm.then_inc(up_done, 1)

        def downs(pe, m, w, weights, order, todo, first_unit=False):
            for n in todo:
                b, k = order[n // len(THREE)]
                q, s = THREE[n % len(THREE)]
                first, lastk = k == 0 and n % len(THREE) == 0, k == JC - 1 and n % len(THREE) == 2
                if first:
                    if first_unit:
                        pe.wait_ge(acc_set, m * B + (b + 1))
                    else:
                        pe.wait_ge(added, unit_no(m, w) * B + (b + 2 - B))
                if n % len(THREE) == 0:
                    pe.wait_ge(hid_ready, chunk_no(m, w, k) + 1)
                mm = nc.tensor.matmul(db[b][:, :], hid[:, k, s, b * TB:(b + 1) * TB], weights(q, k),
                                      start=first, stop=lastk)
                if lastk:
                    mm.then_inc(down_done, 1)

        H_ORDER = [(b, k) for b in range(B) for k in range(JC - 1)] + [(b, JC - 1) for b in range(B)]
        E_ORDER = [(b, k) for b in range(B) for k in range(JC)]
        DOWNS = B * JC * len(THREE)

        def pe_half(pe, m, h, step0, rnn=True):
            ups = 2 * JC * KC * len(THREE)
            for s in range(HSTEPS):
                if rnn:
                    pe_step(pe, step0 + s, s % 2)
                if s < UP_H:
                    half_ups(pe, m, h, range(s * ups // UP_H, (s + 1) * ups // UP_H))
                else:
                    r = HSTEPS - UP_H
                    if s == UP_H:
                        pe.wait_ge(s2_in, (m * HALVES + h + 1) * 16)
                    downs(pe, m, h, lambda q, k: s2[:, q * PART + k * C:q * PART + (k + 1) * C], H_ORDER,
                          range((s - UP_H) * DOWNS // r, (s - UP_H + 1) * DOWNS // r), first_unit=(h == 0))

        def pe_expert(pe, m, e, step0, rnn=True):
            ups = JC * KC * len(THREE)
            for s in range(ESTEPS):
                if rnn:
                    pe_step(pe, step0 + s, s % 2)
                if s < UP_E:
                    expert_ups(pe, e, range(s * ups // UP_E, (s + 1) * ups // UP_E))
                else:
                    r = ESTEPS - UP_E
                    downs(pe, m, e + HALVES,
                          lambda q, k: we2[:, ds(e * (2 * PART) + (q * PART + k * C), C)], E_ORDER,
                          range((s - UP_E) * DOWNS // r, (s - UP_E + 1) * DOWNS // r))

        @block.tensor
        def _(pe):
            pe.wait_ge(consts, E + 4)
            pe.wait_ge(small_in, 16 * (4 + B))
            for b in range(B):
                for k in range(KC):
                    last = nc.tensor.matmul(rbk[0:1, b * E:(b + 1) * E], ct[:, k, b, :], rw[:, KC + k, :],
                                            start=(k == 0), stop=(k == KC - 1))
            last.then_inc(t_ps, 1)
            pe.wait_ge(t_row, 1)
            pe_inputs(pe, 0)
            pe.wait_ge(w_split, 1)
            pe_xw(pe, 0)
            pe.wait_ge(w_split, 2)
            pe.wait_ge(seeded, 2)
            with pe.Fori(0, TB // SL) as g:
                for s in range(SL):
                    pe_step(pe, g * SL + s, s % 2)
            with pe.Fori(1, NB) as i:
                pe_inputs(pe, i)
                pe_rows(pe, i - 1)
                pe_xw(pe, i)
                pe.wait_ge(seeded, i * (TB + 2) + 2)
                pe.wait_ge(x1p_ready, i)
                for h in range(HALVES):
                    pe_half(pe, i - 1, h, i * TB + h * HSTEPS)
                with pe.Fori(0, E) as e:
                    pe_expert(pe, i - 1, e, i * TB + e * ESTEPS + HALVES * HSTEPS)
            pe_rows(pe, NB - 1)
            pe.wait_ge(nlog_ready, NB)
            pe.wait_ge(x1p_ready, NB)
            for h in range(HALVES):
                pe_half(pe, NB - 1, h, 0, rnn=False)
            with pe.Fori(0, E) as e:
                pe_expert(pe, NB - 1, e, 0, rnn=False)

        def act_step(act, n, t, par):
            act.wait_ge(pre_ready, n + 1)
            nc.scalar.activation(hp[:, :, 0, :, :], pre[:, :, :, :], ACT.Tanh, scale=1.0 / WS).then_inc(h_hi, 1)
            nc.scalar.activation(hist[:, :, :, ds(t, 1)], pre[:, :, :, :], ACT.Tanh, scale=1.0 / WS)\
              .then_inc(h_kept, 1)
            act_seed(t + 2, par)

        def act_seed(t, par):
            nc.scalar.activation(z[par][:, :, 2, :], xw[:, :, :, ds(t, 1)].rearrange("p j b o -> p j (b o)"),
                                 ACT.Copy).then_inc(seeded, 1)

        def act_inputs(act, i):
            for c in range(2):
                act.wait_ge(xt_ps, i * 2 + (c + 1))
                nc.scalar.activation(xt[:, 2 * c:2 * c + 2, :].rearrange("p k n -> p (k n)"), ub[c][:, :], ACT.Copy)\
                  .then_inc(xt_ready, 1)
            act.wait_ge(xt_ready, (i + 1) * 2)
            nc.scalar.activation(xp[:, 0, :, :], xt[:, :, :], ACT.Copy).then_inc(xp_hi, 1)

        def act_xw(act, i):
            for j in range(KC):
                act.wait_ge(xw_ps, i * KC + (j + 1))
                nc.scalar.activation(xw[:, j, :, 0:TB], ub[XW_BANK[j]][:, 0:N].rearrange("p (b t) -> p b t", b=B),
                                     ACT.Identity, bias=b64[:, j:j + 1]).then_inc(xw_ready, 1)
            act.wait_ge(xw_ready, (i + 1) * KC)
            for t in range(2):
                act_seed(t, t)

        def act_rows(act, m):
            act.wait_ge(x1_ready, m + 1)
            nc.scalar.activation(x1p[:, 0, :, :], x1[:, :, :], ACT.Copy).then_inc(x1_hi, 1)
            act.wait_ge(acc_free, (m + 1) * 16)
            for b in range(B):
                act.wait_ge(x1_rows, m * B + (b + 1))
                nc.scalar.activation(acc[:, b, :], db[b][:, :], ACT.Copy).then_inc(acc_set, 1)
            act.wait_ge(logits, m + 1)
            nc.scalar.activation(nlog[:, :], rbk[:, 0:B * E], ACT.Copy, scale=-1.0).then_inc(nlog_ready, 1)

        def act_gate(act, m, w, j, bank_no, func, scale):
            act.wait_ge(up_done, chunk_no(m, w, j) + 1)
            nc.scalar.activation(et[:, j % 2, :], ub[bank_no][:, 0:N], func, scale=scale).then_inc(act_done, 1)

        def act_hi(act, m, w, j, g, scale, done):
            act.wait_ge(done, (m * (HALVES * JC) + w * JC + j if done is g_done else chunk_no(m, w, j)) + 1)
            nc.scalar.activation(hid[:, j, 0, :], g[:, j % 2, :], ACT.Copy, scale=scale).then_inc(hid_hi, 1)

        H_GATE = {3 * (j + 1): j for j in range(JC)}
        E_GATE = {2: 0, 3: 1, 5: 2, 6: 3}

        def act_half(act, m, h, step0, t0, rnn=True):
            for s in range(HSTEPS):
                if rnn:
                    act_step(act, step0 + s, t0 + s, s % 2)
                if s in H_GATE:
                    act_gate(act, m, h, H_GATE[s], 2 * (H_GATE[s] % 2), ACT.Tanh, 0.5 / WS)
                if s - 1 in H_GATE:
                    act_hi(act, m, h, H_GATE[s - 1], gt, 1.0, g_done)

        def act_expert(act, m, e, step0, t0, rnn=True):
            for s in range(ESTEPS):
                if rnn:
                    act_step(act, step0 + s, t0 + s, s % 2)
                if s - 1 in E_GATE:
                    act_hi(act, m, e + HALVES, E_GATE[s - 1], et, GS, act_done)
                if s in E_GATE:
                    if E_GATE[s] >= 2:
                        act.wait_ge(hid_ready, chunk_no(m, e + HALVES, E_GATE[s] - 2) + 1)
                    act_gate(act, m, e + HALVES, E_GATE[s], E_GATE[s], ACT.Gelu, 1.0 / WS)

        def split_hi(act, dst, src):
            nc.scalar.activation(dst, src, ACT.Copy, scale=WS).then_inc(w_hi, 1)

        @block.scalar
        def _(act):
            n = PART // SL
            act.wait_ge(consts, E + 4)
            act.wait_ge(small_in, 16 * (4 + B))
            nc.scalar.activation(hp[:, :, 0, :, :], ct[:, :, :, :], ACT.Gelu).then_inc(h0_hi, 1)
            act.wait_ge(h0_hi, 1)
            nc.scalar.activation(hp[:, :, 0, :, :], ct[:, :, :, :], ACT.Copy).then_inc(h_hi, 1)
            act.wait_ge(t_ps, 1)
            nc.scalar.activation(trow[0:1, :], rbk[0:1, 0:B * E], ACT.Copy).then_inc(t_row, 1)
            act_inputs(act, 0)
            for g, w in enumerate((wx, wh)):
                act.wait_ge(wxh_in, 16 * 2)
                nc.scalar.activation(w[:, 0:PART], stage[:, g, :], ACT.Copy, scale=WS).then_inc(w_hi, 1)
            act.wait_ge(b_scaled, 1)
            act_xw(act, 0)
            for g in range(NSH):
                act.wait_ge(staged[g % 2], 16 * (g // 2 + 1))
                for s in range(SL):
                    act_step(act, g * SL + s, g * SL + s, s % 2)
                    o = (2 + g) * 2 * PART + s * n
                    split_hi(act, we2[:, o:o + n], stage[:, g % 2, s * n:(s + 1) * n])
            with act.Fori(0, E) as e:
                for c, w in enumerate((we1, we2)):
                    act.wait_ge(staged[c], e * 16 + 16 * (NSH // 2 + 1))
                    for s in range(SL):
                        t = e * (2 * SL) + (NSH * SL + c * SL + s)
                        act_step(act, t, t, s % 2)
                        if c == 1 and s == 0:
                            act.wait_ge(scratch_out, 16 * (2 * HALVES * JC + HALVES))
                        split_hi(act, w[:, ds(e * (2 * PART) + s * n, n)], stage[:, c, s * n:(s + 1) * n])
            with act.Fori((NSH + NEX), TB // SL) as g:
                for s in range(SL):
                    act_step(act, g * SL + s, g * SL + s, s % 2)
            with act.Fori(1, NB) as i:
                act.wait_ge(x1_ready, i)
                act_inputs(act, i)
                act_rows(act, i - 1)
                act_xw(act, i)
                for h in range(HALVES):
                    act_half(act, i - 1, h, i * TB + h * HSTEPS, h * HSTEPS)
                with act.Fori(0, E) as e:
                    act_expert(act, i - 1, e, i * TB + e * ESTEPS + HALVES * HSTEPS,
                               e * ESTEPS + HALVES * HSTEPS)
            act_rows(act, NB - 1)
            for h in range(HALVES):
                act_half(act, NB - 1, h, 0, 0, rnn=False)
            with act.Fori(0, E) as e:
                act_expert(act, NB - 1, e, 0, 0, rnn=False)

        def dve_step(dve, n, t, par):
            dve.wait_ge(z_ready, n + 1)
            nc.vector.tensor_reduce(pre[:, :, :, 0], z[par].rearrange("p j c b -> p j b c"), axis=AX.X, op=ALU.add)\
              .then_inc(pre_ready, 1)
            dve.wait_ge(h_hi, n + 2)
            dve.wait_ge(h_kept, n + 1)
            nc.vector.tensor_tensor(hp[:, :, 1, :, :], hist[:, :, :, ds(t, 1)], hp[:, :, 0, :, :], ALU.subtract)\
              .then_inc(h_ready, 1)

        def dve_inputs(dve, i):
            dve.wait_ge(xp_hi, i + 1)
            nc.vector.tensor_tensor(xp[:, 1, :, :], xt[:, :, :], xp[:, 0, :, :], ALU.subtract).then_inc(xp_ready, 1)

        CHAIN = 26

        def dve_gates(dve, m):
            count = [0]

            def link(ins):
                count[0] += 1
                ins.then_inc(chain, 1)
                dve.wait_ge(chain, m * CHAIN + count[0])

            def pick(onehot):
                link(nc.vector.tensor_reduce(mx[:, :, 0], sel[:, :, :], axis=AX.X, op=ALU.max))
                link(nc.vector.tensor_tensor(m1[:, :, :], sel[:, :, :], mx[:, :, :].to_broadcast([P, B, E]),
                                             ALU.is_ge))
                link(nc.vector.tensor_tensor(m1[:, :, :], m1[:, :, :], rev[:, :, :], ALU.mult))
                link(nc.vector.tensor_reduce(mx[:, :, 0], m1[:, :, :], axis=AX.X, op=ALU.max))
                link(nc.vector.tensor_tensor(onehot[:, :, :], m1[:, :, :], mx[:, :, :].to_broadcast([P, B, E]),
                                             ALU.is_equal))

            dve.wait_ge(pow_ready, m + 1)
            link(nc.vector.tensor_scalar(pw[:, :], pw[:, :], 1.0, None, ALU.add))
            link(nc.vector.reciprocal(sg[:, :, :].rearrange("p b e -> p (b e)"), pw[:, :]))
            link(nc.vector.tensor_tensor(sel[:, :, :], sg[:, :, :], rb[:, :, :], ALU.add))
            pick(oh1)
            link(nc.vector.scalar_tensor_tensor(out=sel[:, :, :], in0=oh1[:, :, :], scalar=-BIG, in1=sel[:, :, :],
                                                op0=ALU.mult, op1=ALU.add))
            pick(oh2)
            link(nc.vector.tensor_tensor(m1[:, :, :], oh1[:, :, :], oh2[:, :, :], ALU.add))
            link(nc.vector.tensor_tensor(oh1[:, :, :], m1[:, :, :], sg[:, :, :], ALU.mult))
            link(nc.vector.tensor_reduce(den[:, :, 0], oh1[:, :, :], axis=AX.X, op=ALU.add))
            link(nc.vector.tensor_scalar(okd[:, :, :], den[:, :, :], 1e-9, OS, ALU.is_gt, ALU.mult))
            link(nc.vector.tensor_scalar(alt[:, :, :], okd[:, :, :], -0.5, 0.5 * OS, ALU.mult, ALU.add))
            link(nc.vector.tensor_scalar(den[:, :, :], den[:, :, :], 1e-9, None, ALU.add))
            link(nc.vector.reciprocal(den[:, :, :], den[:, :, :]))
            link(nc.vector.tensor_tensor(den[:, :, :], den[:, :, :], okd[:, :, :], ALU.mult))
            for b in range(B):
                link(nc.vector.tensor_scalar(oh2[:, b, :], m1[:, b, :], alt[:, b, :], None, ALU.mult))
            for b in range(B):
                link(nc.vector.scalar_tensor_tensor(out=gates[:, b * E:(b + 1) * E], in0=oh1[:, b, :],
                                                    scalar=den[:, b, :], in1=oh2[:, b, :],
                                                    op0=ALU.mult, op1=ALU.add))
            assert count[0] == CHAIN

        def dve_x1(dve, m):
            dve.wait_ge(h_kept, (m + 1) * TB)
            nc.vector.tensor_tensor(x1[:, :, :], xt[:, :, :], hist[:, :, :, :].rearrange("p k b t -> p k (b t)"),
                                    ALU.add).then_inc(x1_ready, 1)

        def dve_rows(dve, m):
            dve.wait_ge(x1_hi, m + 1)
            nc.vector.tensor_tensor(x1p[:, 1, :, :], x1[:, :, :], x1p[:, 0, :, :], ALU.subtract)\
              .then_inc(x1p_ready, 1)
            dve_gates(dve, m)

        def dve_silu(dve, m, h, j):
            a, b = ub[2 * (j % 2)][:, 0:N], ub[2 * (j % 2) + 1][:, 0:N]
            dve.wait_ge(act_done, chunk_no(m, h, j) + 1)
            nc.vector.scalar_tensor_tensor(out=ut[:, :], in0=et[:, j % 2, :], scalar=1.0, in1=a,
                                           op0=ALU.add, op1=ALU.mult).then_inc(u_done, 1)
            dve.wait_ge(u_done, m * (HALVES * JC) + (h * JC + j + 1))
            nc.vector.scalar_tensor_tensor(out=gt[:, j % 2, :], in0=ut[:, :], scalar=GS / (2.0 * WS * WS), in1=b,
                                           op0=ALU.mult, op1=ALU.mult).then_inc(g_done, 1)

        def dve_lo(dve, m, w, j, g, scale):
            dve.wait_ge(hid_hi, chunk_no(m, w, j) + 1)
            nc.vector.scalar_tensor_tensor(out=hid[:, j, 1, :], in0=g[:, j % 2, :], scalar=scale,
                                           in1=hid[:, j, 0, :], op0=ALU.mult, op1=ALU.subtract)\
               .then_inc(hid_ready, 1)

        def dve_add(dve, m, w, b, scalar):
            dve.wait_ge(down_done, unit_no(m, w) * B + (b + 1))
            nc.vector.scalar_tensor_tensor(out=acc[:, b, :], in0=db[b][:, :], scalar=scalar, in1=acc[:, b, :],
                                           op0=ALU.mult, op1=ALU.add).then_inc(added, 1)

        def dve_half(dve, m, h, step0, t0, rnn=True):
            for s in range(HSTEPS):
                if rnn:
                    dve_step(dve, step0 + s, t0 + s, s % 2)
                if s in H_GATE:
                    dve_silu(dve, m, h, H_GATE[s])
                if s - 1 in H_GATE:
                    dve_lo(dve, m, h, H_GATE[s - 1], gt, 1.0)
                if s == HSTEPS - 1:
                    for b in range(B):
                        dve.wait_ge(added, unit_no(m, h) * B + (b + 1))
                        dve_add(dve, m, h, b, OS)

        def dve_expert(dve, m, e, step0, t0, rnn=True):
            for s in range(ESTEPS):
                if rnn:
                    dve_step(dve, step0 + s, t0 + s, s % 2)
                if s - 1 in E_GATE:
                    dve_lo(dve, m, e + HALVES, E_GATE[s - 1], et, GS)
                for b, at in ((0, UP_E + 3), (1, ESTEPS - 1)):
                    if s == at:
                        dve.wait_ge(added, unit_no(m, e + HALVES) * B + (b + 1))
                        dve_add(dve, m, e + HALVES, b, gates[:, ds(e + b * E, 1)])

        def split_lo(dve, count, dst, hi, src):
            dve.wait_ge(w_hi, count)
            nc.vector.scalar_tensor_tensor(out=dst, in0=src, scalar=WS, in1=hi, op0=ALU.mult, op1=ALU.subtract)\
              .then_inc(w_split, 1)

        @block.vector
        def _(dve):
            n = PART // SL
            dve.wait_ge(consts, E + 4)
            dve.wait_ge(small_in, 16 * (4 + B))
            nc.vector.tensor_scalar(b64[:, :], b64[:, :], WS, None, ALU.mult).then_inc(b_scaled, 1)
            nc.vector.memset(gates[:, :], 0.0).then_inc(added, 1)
            dve.wait_ge(h_hi, 1)
            nc.vector.tensor_tensor(hp[:, :, 1, :, :], ct[:, :, :, :], hp[:, :, 0, :, :], ALU.subtract)\
              .then_inc(h_ready, 1)
            dve_inputs(dve, 0)
            for g, w in enumerate((wx, wh)):
                split_lo(dve, g + 1, w[:, PART:2 * PART], w[:, 0:PART], stage[:, g, :])
            dve.wait_ge(xw_ready, KC)
            for g in range(NSH):
                for s in range(SL):
                    dve_step(dve, g * SL + s, g * SL + s, s % 2)
                    o = (2 + g) * 2 * PART + s * n
                    split_lo(dve, 2 + g * SL + s + 1, we2[:, PART + o:PART + o + n], we2[:, o:o + n],
                             stage[:, g % 2, s * n:(s + 1) * n])
            with dve.Fori(0, E) as e:
                for c, w in enumerate((we1, we2)):
                    for s in range(SL):
                        t = e * (2 * SL) + (NSH * SL + c * SL + s)
                        dve_step(dve, t, t, s % 2)
                        split_lo(dve, t + 3, w[:, ds(e * (2 * PART) + (PART + s * n), n)],
                                 w[:, ds(e * (2 * PART) + s * n, n)], stage[:, c, s * n:(s + 1) * n])
            with dve.Fori((NSH + NEX), TB // SL) as g:
                for s in range(SL):
                    dve_step(dve, g * SL + s, g * SL + s, s % 2)
            with dve.Fori(1, NB) as i:
                dve_x1(dve, i - 1)
                dve_inputs(dve, i)
                dve_rows(dve, i - 1)
                dve.wait_ge(acc_set, i * B)
                dve.wait_ge(xw_ready, (i + 1) * KC)
                for h in range(HALVES):
                    dve_half(dve, i - 1, h, i * TB + h * HSTEPS, h * HSTEPS)
                with dve.Fori(0, E) as e:
                    dve_expert(dve, i - 1, e, i * TB + e * ESTEPS + HALVES * HSTEPS,
                               e * ESTEPS + HALVES * HSTEPS)
            dve_x1(dve, NB - 1)
            dve_rows(dve, NB - 1)
            dve.wait_ge(acc_set, NB * B)
            for h in range(HALVES):
                dve_half(dve, NB - 1, h, 0, 0, rnn=False)
            with dve.Fori(0, E) as e:
                dve_expert(dve, NB - 1, e, 0, 0, rnn=False)


_INS = ["x", "cond_1024", "L0_cond_Wx", "L0_cond_Wh", "L0_cond_b", "L1_cond_router_W", "L1_cond_router_bias",
        "L1_cond_w1", "L1_cond_w3", "L1_cond_w2", "L1_cond_W1e", "L1_cond_W2e"]


def kernel(**inputs):
    import numpy as _np
    import concourse.bacc as _bacc
    from concourse import mybir as _mybir
    from concourse.bass_utils import run_bass_kernel_spmd as _run

    nc = _bacc.Bacc("TRN2", target_bir_lowering=False, num_devices=1)
    arrays, args = {}, []
    for name in _INS:
        a = _np.ascontiguousarray(inputs[name])
        arrays[f"in_{name}"] = a
        args.append(nc.dram_tensor(f"in_{name}", a.shape, _mybir.dt.from_np(a.dtype), kind="ExternalInput").ap())
    shape = inputs["x"].shape
    args.append(nc.dram_tensor("out_0", shape, _mybir.dt.float32, kind="ExternalOutput").ap())
    rnn_then_moe_kernel(nc, *args)
    r = _run(nc, [arrays], core_ids=[0])
    return r.results[0]["out_0"]
```

```python
import math

import concourse.bass as bass
from concourse import mybir
from contextlib import ExitStack


def rnn_then_moe_kernel(
    nc: bass.Bass,
    x: bass.AP,
    cond: bass.AP,
    Wx: bass.AP,
    Wh: bass.AP,
    b_rnn: bass.AP,
    router_W: bass.AP,
    router_bias: bass.AP,
    w1: bass.AP,
    w3: bass.AP,
    w2: bass.AP,
    W1e: bass.AP,
    W2e: bass.AP,
    out: bass.AP,
):
    f32 = mybir.dt.float32
    f16 = mybir.dt.float16
    ALU = mybir.AluOpType
    ACT = mybir.ActivationFunctionType
    AX = mybir.AxisListType
    ds = bass.ds

    P = 128
    B, T, C = x.shape
    E, _, HE = W1e.shape
    HS = w1.shape[1]
    TB = P
    NB = T // TB
    KC = C // P
    N = B * TB
    HALVES = HS // HE
    JC = HE // P
    UNITS = HALVES + E
    CH = UNITS * JC
    PART = KC * C
    WS = 64.0
    GS = 2.0 * WS
    OS = 1.0 / (3.0 * GS * WS)
    ESTEPS = 12
    H0 = [0, 17, TB - E * ESTEPS]
    HSTEPS = [H0[1] - H0[0], H0[2] - H0[1]]
    UPS = [[0, 10, 18, 26, 35, 44, 50, 59, 68, 77, 86, 96], [(s + 1) * 96 // 10 for s in range(10)]]
    UP_E = ESTEPS // 2
    SL = 4
    NSH = 3 * HALVES
    NEX = 2 * E
    BIG = 1.0e30
    XS = 2 * SL
    PIECES = HALVES + E
    TC = TB - ESTEPS
    LEAD = 2
    X1P = 3
    G = KC * B

    sc13 = nc.dram_tensor("shared_up_parts", [HALVES * JC, P, 2, 2, KC, P], f16).ap()
    xts = nc.dram_tensor("x_channels", [NB, P, KC * N], f32).ap()
    xws = nc.dram_tensor("xw_channels", [P, G, LEAD + T + 2], f32).ap()
    sc2 = nc.dram_tensor("shared_down_parts", [HALVES, P, 2 * PART], f16).ap()

    ctx = ExitStack()
    with ctx:
        def sb(name, shape, dt):
            return ctx.enter_context(nc.sbuf_tensor(name, shape, dt))

        def sem(name):
            return ctx.enter_context(nc.semaphore(name))

        wx = sb("wx", [P, 2 * PART], f16)
        wh = sb("wh", [P, 2 * PART], f16)
        we1 = sb("we1", [P, E * 2 * PART], f16)
        we2 = sb("we2", [P, E * 2 * PART], f16)
        stream = sb("stream", [P, 2 * PART], f32)
        s13 = stream[:, 0:PART].bitcast(f16).rearrange("p (s w q k c) -> p s w q k c", s=2, w=2, q=2, k=KC)
        s2 = stream[:, PART:2 * PART].bitcast(f16)
        stage = stream[:, :].rearrange("p (s n) -> p s n", s=2)
        hp = sb("hp", [P, KC, 2, B, 1], f16)
        hist = sb("hist", [P, KC, B, TB], f32)
        xw = sb("xw", [P, KC, B, TB], f32)
        xw0 = sb("xw0", [P, KC, B, 2], f32)
        pre = sb("pre", [P, KC, B, 1], f32)
        xn = sb("xn", [P, B, C], f32)
        xt = sb("xt", [P, KC, N], f32)
        xp = sb("xp", [P, 2, KC, N], f16)
        x1 = sb("x1", [P, KC, N], f32)
        x1p = sb("x1p", [P, 2, KC, N], f16)
        et = sb("et", [P, 2, N], f32)
        ut = sb("ut", [P, N], f32)
        gt = sb("gt", [P, 2, N], f32)
        hid = sb("hid", [P, JC, 2, N], f16)
        acc = sb("acc", [P, B, C], f32)
        pad = sb("pad", [P, G, 2], f32)
        ident = sb("ident", [P, P], f32)
        ones = sb("ones", [1, P], f16)
        ct = sb("ct", [P, KC, B, 1], f32)
        b64 = sb("b64", [P, KC], f32)
        rw = sb("rw", [P, 2 * KC, E], f32)
        rwp = sb("rwp", [P, 2, KC, E], f16)
        rb = sb("rb", [P, B, E], f32)
        rev = sb("rev", [P, B, E], f32)
        trow = sb("trow", [1, B * E], f32)
        trp = sb("trp", [1, 2, B * E], f16)
        base = sb("base", [P, B * E], f32)
        nlog = sb("nlog", [P, B * E], f32)
        pw = sb("pw", [P, B * E], f32)
        sg = sb("sg", [P, B, E], f32)
        sel = sb("sel", [P, B, E], f32)
        m1 = sb("m1", [P, B, E], f32)
        oh1 = sb("oh1", [P, B, E], f32)
        oh2 = sb("oh2", [P, B, E], f32)
        mx = sb("mx", [P, B, 1], f32)
        den = sb("den", [P, B, 1], f32)
        okd = sb("okd", [P, B, 1], f32)
        alt = sb("alt", [P, B, 1], f32)
        gates = sb("gates", [P, B * (1 + E)], f32)

        def bank(name):
            return ctx.enter_context(nc.psum_tensor(name, [P, 512], f32))

        zb = [bank(f"zb{i}") for i in range(2)]
        ub = [bank(f"ub{i}") for i in range(4)]
        db = [bank(f"db{i}") for i in range(2)]
        rbk = ub[3]
        z = [zb[i][:, 0:KC * 3 * B].rearrange("p (j c b) -> p j c b", j=KC, c=3) for i in range(2)]

        small_in = sem("small_in")
        x_in = sem("x_in")
        xw_in = [sem("xw_in0"), sem("xw_in1")]
        xt_in = sem("xt_in")
        tail_in = sem("tail_in")
        pad_out = sem("pad_out")
        xt_out = sem("xt_out")
        wxh_in = [sem("wx_in"), sem("wh_in")]
        staged = [sem("staged0"), sem("staged1")]
        s13_in = [sem("s13_in0"), sem("s13_in1")]
        s2_in = sem("s2_in")
        scratch_out = sem("scratch_out")
        acc_free = sem("acc_free")
        consts = sem("consts")
        ident0 = sem("ident0")
        b_scaled = sem("b_scaled")
        h0_hi = sem("h0_hi")
        t_ps = sem("t_ps")
        t_row = sem("t_row")
        rw_hi = sem("rw_hi")
        rw_split = sem("rw_split")
        w_hi = sem("w_hi")
        w_split = sem("w_split")
        z_ready = sem("z_ready")
        seeded = sem("seeded")
        pre_ready = sem("pre_ready")
        h_kept = sem("h_kept")
        h_hi = sem("h_hi")
        h_ready = sem("h_ready")
        xt_ps = sem("xt_ps")
        xt_ready = sem("xt_ready")
        xp_hi = sem("xp_hi")
        xp_ready = sem("xp_ready")
        xw_ps = sem("xw_ps")
        xw_ready = sem("xw_ready")
        xw0_ready = sem("xw0_ready")
        x1_ready = sem("x1_ready")
        x1_hi = sem("x1_hi")
        x1p_ready = sem("x1p_ready")
        x1_rows = sem("x1_rows")
        acc_set = sem("acc_set")
        logits = sem("logits")
        nlog_ready = sem("nlog_ready")
        pow_ready = sem("pow_ready")
        chain = sem("chain")
        up_done = sem("up_done")
        act_done = sem("act_done")
        u_done = sem("u_done")
        g_done = sem("g_done")
        hid_hi = sem("hid_hi")
        hid_ready = sem("hid_ready")
        down_done = sem("down_done")
        added = sem("added")

        block = ctx.enter_context(nc.Block())

        def chunk_no(m, w, j):
            return m * CH + w * JC + j

        def unit_no(m, w):
            return m * UNITS + w

        XW_BANK = [2, 0, 1, 3]

        def to_scratch(sp, g):
            sp.wait_ge(w_split, 2 + SL * (g + 1))
            src = we2[:, (2 + g) * 2 * PART:(3 + g) * 2 * PART]
            if g < 2 * HALVES:
                w, h = g // HALVES, g % HALVES
                parts = src.rearrange("p (g n) -> p g n", n=C)
                for j in range(JC):
                    sp.dma_start(sc13[h * JC + j, :, w, :, :, :].rearrange("p q k c -> p (q k) c"),
                                 parts[:, :, j * P:(j + 1) * P]).then_inc(scratch_out, 16)
            else:
                sp.dma_start(sc2[g - 2 * HALVES, :, :], src).then_inc(scratch_out, 16)

        def x_block(sp, i):
            sp.wait_ge(xt_ps, i * 2)
            sp.dma_start(xn[:, :, :], x[:, ds(i * TB, TB), :].rearrange("b t c -> t b c")).then_inc(x_in, 16)

        def up_weights(sp, h, j):
            sp.dma_start(s13[:, j % 2, :, :, :, :].rearrange("p w q k c -> p (w q k c)"),
                         sc13[h * JC + j, :, :, :, :, :].rearrange("p w q k c -> p (w q k c)"))\
              .then_inc(s13_in[j % 2], 16)

        def down_weights(sp, h):
            sp.dma_start(s2, sc2[h, :, :]).then_inc(s2_in, 16)

        def first_weights(sp):
            for j in range(2):
                up_weights(sp, 0, j)
            down_weights(sp, 0)

        def weights(sp, m, last=False):
            for h in range(HALVES):
                for j in range(JC):
                    hn, jn = (h, j + 2) if j + 2 < JC else (h + 1, j + 2 - JC)
                    if hn == HALVES and last:
                        continue
                    sp.wait_ge(up_done, chunk_no(m, h, j) + 1)
                    up_weights(sp, hn % HALVES, jn)
                if h < HALVES - 1 or not last:
                    sp.wait_ge(down_done, (unit_no(m, h) + 1) * B)
                    down_weights(sp, (h + 1) % HALVES)

        def xw_half(sp, i, c):
            n = TB // 2
            sp.wait_ge(seeded, (i - 1) * TB + ((c + 1) * n + 2))
            sp.dma_start(xw[:, :, :, c * n:(c + 1) * n].rearrange("p k b t -> p (k b) t"),
                         xws[:, :, ds(i * TB + (LEAD + 2 + c * n), n)]).then_inc(xw_in[c], 16)

        def block_dma(sp, i, last=False):
            xw_half(sp, i, 1)
            sp.wait_ge(x1_ready, i * PIECES)
            sp.dma_start(xt[:, :, :].rearrange("p k n -> p (k n)"),
                         xts.rearrange("i p n -> (i p) n")[ds(i * P, P), :]).then_inc(xt_in, 16)
            weights(sp, i - 1)
            if not last:
                xw_half(sp, i + 1, 0)
            block_out(sp, i - 1)

        def block_out(sp, m):
            sp.wait_ge(added, (m + 1) * (UNITS * B) + 1)
            sp.dma_start(out[:, ds(m * TB, TB), :].rearrange("b t c -> t b c"), acc[:, :, :]).then_inc(acc_free, 16)

        def k_rows(w, r0, c0):
            return w[r0:r0 + C, c0:c0 + C].rearrange("(k p) n -> p k n", p=P)

        def stage_shared(sp, g):
            jobs = [k_rows(w, 0, h * HE) for w in (w1, w3) for h in range(HALVES)]
            jobs += [k_rows(w2, h * HE, 0) for h in range(HALVES)]
            sp.wait_ge(w_split, 2 + (SL * (g - 1) if g >= 2 else g - 1))
            sp.dma_start(stage[:, g % 2, :].rearrange("p (k n) -> p k n", k=KC), jobs[g]).then_inc(staged[g % 2], 16)

        def stage_expert(sp, e, c):
            sp.wait_ge(w_split, e * (2 * SL) + (2 + SL * (NSH - 1 + c)))
            sp.dma_start(stage[:, c, :].rearrange("p (k n) -> p k n", k=KC),
                         (W1e, W2e)[c].rearrange("e r n -> (e r) n")[ds(e * C, C), :]
                         .rearrange("(k p) n -> p k n", p=P)).then_inc(staged[c], 16)

        def store_x(sp, i):
            sp.wait_ge(xt_ready, (i + 1) * 2)
            sp.dma_start(xts.rearrange("i p n -> (i p) n")[ds(i * P, P), :],
                         x1[:, :, :].rearrange("p k n -> p (k n)")).then_inc(xt_out, 16)

        def store_xw(sp, i):
            sp.wait_ge(xw_ready, (i + 1) * KC)
            sp.dma_start(xws[:, :, ds(i * TB + LEAD, TB)], acc[:, :, :].rearrange("p b c -> p (b c)")
                         .rearrange("p (g t) -> p g t", t=TB)).then_inc(acc_free, 16)

        @block.sync
        def _(sp):
            x_block(sp, 0)
            with nc.allow_non_contiguous_dma(reason="a few KB of constants, once"):
                sp.dma_start(b64[:, :], b_rnn.rearrange("(k p) -> p k", p=P)).then_inc(small_in, 16)
                for b in range(B):
                    sp.dma_start(ct[:, :, b, 0], cond[b, :].rearrange("(k p) -> p k", p=P)).then_inc(small_in, 16)
            sp.dma_start(stage[:, 0, :].rearrange("p (k n) -> p k n", k=KC), k_rows(Wx, 0, 0)).then_inc(wxh_in[0], 16)
            sp.dma_start(stage[:, 1, :].rearrange("p (k n) -> p k n", k=KC), k_rows(Wh, 0, 0)).then_inc(wxh_in[1], 16)
            with nc.allow_non_contiguous_dma(reason="a few KB of constants, once"):
                sp.dma_start(rw[:, :, :], router_W.rearrange("(k p) e -> p k e", p=P)).then_inc(small_in, 16)
                for b in range(B):
                    sp.dma_start(rb[:, b, :], router_bias.rearrange("(o e) -> o e", o=1).to_broadcast([P, E]))\
                      .then_inc(small_in, 16)
            x_block(sp, 1)
            stage_shared(sp, 0)
            stage_shared(sp, 1)
            for u in range(NSH // 2):
                x_block(sp, u + 2)
                for c in range(2):
                    if 2 * u + 2 + c < NSH:
                        stage_shared(sp, 2 * u + 2 + c)
                    else:
                        stage_expert(sp, 0, c)
                    to_scratch(sp, 2 * u + c)
                    (store_x, store_xw)[c](sp, u + 1)
                if u == 0:
                    sp.wait_ge(consts, E + 4)
                    sp.dma_start(xws[:, :, LEAD + T:LEAD + T + 2], pad[:, :, :]).then_inc(pad_out, 16)
                    sp.wait_ge(acc_free, 16)
                    sp.dma_start(xw[:, :, :, TB - 2:TB].rearrange("p k b t -> p (k b) t"), xws[:, :, LEAD + TB:LEAD + TB + 2])\
                      .then_inc(tail_in, 16)
            with sp.Fori(1, E) as e:
                x_block(sp, e + (NSH // 2 + 1))
                stage_expert(sp, e, 0)
                store_x(sp, e + NSH // 2)
                stage_expert(sp, e, 1)
                store_xw(sp, e + NSH // 2)
            with sp.Fori(NSH // 2 + E, NB - 1) as i:
                x_block(sp, i + 1)
                store_x(sp, i)
                store_xw(sp, i)
            store_x(sp, NB - 1)
            store_xw(sp, NB - 1)
            sp.wait_ge(w_split, 2 + SL * (NSH + NEX))
            sp.wait_ge(scratch_out, 16 * (2 * HALVES * JC + HALVES))
            first_weights(sp)
            sp.wait_ge(acc_free, (NB - 1) * 16)
            sp.wait_ge(xt_out, (NB - 1) * 16)
            sp.wait_ge(pad_out, 16)
            xw_half(sp, 1, 0)
            with sp.Fori(1, NB - 1) as i:
                block_dma(sp, i)
            block_dma(sp, NB - 1, last=True)
            weights(sp, NB - 1, last=True)
            block_out(sp, NB - 1)
            sp.wait_ge(acc_free, (2 * NB - 1) * 16)

        def pool_inputs(pool, i):
            for c in range(2):
                k = slice(2 * c, 2 * c + 2)
                pool.wait_ge(xp_hi, i * 2 + (c + 1))
                nc.gpsimd.tensor_tensor(xp[:, 1, k, :], x1[:, k, :], xp[:, 0, k, :], ALU.subtract)\
                  .then_inc(xp_ready, 1)

        def pool_x1(pool, m, t0, n):
            pool.wait_ge(h_kept, m * TB + t0 + n)
            nc.gpsimd.tensor_tensor(x1[:, :, :].rearrange("p k (b t) -> p (k b) t", b=B)[:, :, ds(t0, n)],
                                    xt[:, :, :].rearrange("p k (b t) -> p (k b) t", b=B)[:, :, ds(t0, n)],
                                    hist[:, :, :, :].rearrange("p k b t -> p (k b) t")[:, :, ds(t0, n)],
                                    ALU.add).then_inc(x1_ready, 1)

        def pool_block(pool, m):
            pool.wait_ge(xt_in, (m + 1) * 16)
            for h in range(HALVES):
                pool_x1(pool, m, H0[h], HSTEPS[h])
            with pool.Fori(0, E - 1) as e:
                pool_x1(pool, m, e * ESTEPS + H0[HALVES], ESTEPS)
            for c in range(2):
                pool_x1p(pool, m, c)
            pool_x1(pool, m, TC, ESTEPS)
            pool_x1p(pool, m, 2)

        def x1_piece(c):
            return [(slice(0, KC), slice(0, TC)), (slice(KC, 2 * KC), slice(0, TC)), (slice(0, G), slice(TC, TB))][c]

        def pool_x1p(pool, m, c):
            g, t = x1_piece(c)
            pool.wait_ge(x1_hi, m * X1P + (c + 1))
            nc.gpsimd.tensor_tensor(x1p[:, 1, :, :].rearrange("p k (b t) -> p (k b) t", b=B)[:, g, t],
                                    x1[:, :, :].rearrange("p k (b t) -> p (k b) t", b=B)[:, g, t],
                                    x1p[:, 0, :, :].rearrange("p k (b t) -> p (k b) t", b=B)[:, g, t],
                                    ALU.subtract).then_inc(x1p_ready, 1)

        def pool_pow(pool, m):
            pool.wait_ge(nlog_ready, m + 1)
            nc.gpsimd.tensor_tensor(pw[:, :], base[:, :], nlog[:, :], ALU.pow).then_inc(pow_ready, 1)

        @block.gpsimd
        def _(pool):
            nc.gpsimd.memset(ones[:, :], 1.0).then_inc(consts, 1)
            nc.gpsimd.memset(pad[:, :, :], 0.0).then_inc(consts, 1)
            nc.gpsimd.memset(base[:, :], math.e).then_inc(consts, 1)
            for e in range(E):
                nc.gpsimd.memset(rev[:, :, e], float(E - e)).then_inc(consts, 1)
            nc.gpsimd.memset(ident[:, :], 0.0).then_inc(ident0, 1)
            pool.wait_ge(ident0, 1)
            nc.gpsimd.affine_select(out=ident[:, :], in_=ident[:, :], compare_op=ALU.not_equal, fill=1.0, base=0,
                                    pattern=[[-1, P]], channel_multiplier=1).then_inc(consts, 1)
            with pool.Fori(1, NB) as i:
                pool_inputs(pool, i)
            pool.wait_ge(xt_out, (NB - 1) * 16)
            pool.wait_ge(xp_ready, NB * 2)
            pool_block(pool, 0)
            with pool.Fori(1, NB) as i:
                pool_pow(pool, i - 1)
                pool_block(pool, i)
            pool_pow(pool, NB - 1)

        THREE = ((0, 0), (0, 1), (1, 0))

        def wpart(w, q, k, c0, n):
            return w[:, q * PART + k * C + c0:q * PART + k * C + c0 + n]

        def pe_step(pe, n, par):
            pe.wait_ge(h_hi, n + 1)
            for j in range(KC):
                for k in range(KC):
                    nc.tensor.matmul(z[par][:, j, 0, :], wpart(wh, 1, k, j * P, P), hp[:, k, 0, :, 0],
                                     start=(j == 0 and k == 0), stop=False, skip_group_check=True)
            pe.wait_ge(h_ready, n + 1)
            for j in range(KC):
                for k in range(KC):
                    last = nc.tensor.matmul(z[par][:, j, 0:2, :], wpart(wh, 0, k, j * P, P), hp[:, k, :, :, 0],
                                            start=False, stop=(k == KC - 1), skip_group_check=True)
            last.then_inc(z_ready, 1)

        def pe_inputs(pe, i, c):
            if c == 0:
                pe.wait_ge(x_in, (i + 1) * 16)
            if not (isinstance(i, int) and i == 0):
                pe.wait_ge(xt_ready, i * 2)
            for k in range(2 * c, 2 * c + 2):
                for b in range(B):
                    o = (k % 2) * N + b * TB
                    last = nc.tensor.transpose(db[c][:, o:o + TB], xn[:, b, k * P:(k + 1) * P], ident[:, :])
            last.then_inc(xt_ps, 1)

        XW_ALL = KC * KC * len(THREE)

        def pe_xw(pe, i, todo):
            for n in todo:
                k, r = divmod(n, KC * len(THREE))
                j, t = divmod(r, len(THREE))
                q, u = THREE[t]
                if n == 0 and not (isinstance(i, int) and i == 0):
                    pe.wait_ge(xw_ready, i * KC)
                if r == 0 and k % 2 == 0:
                    pe.wait_ge(xp_ready, i * 2 + (k // 2 + 1))
                mm = nc.tensor.matmul(ub[j][:, 0:N], wpart(wx, q, k, j * P, P), xp[:, u, k, :],
                                      start=(k == 0 and t == 0), stop=(k == KC - 1 and t == 2))
                if k == KC - 1 and t == 2:
                    mm.then_inc(xw_ps, 1)

        def pe_ahead(pe, i, s):
            if s < 2:
                pe_inputs(pe, i, s)
            elif s >= 3:
                pe_xw(pe, i, range((s - 3) * XW_ALL // (XS - 3), (s - 2) * XW_ALL // (XS - 3)))

        def pe_rows(pe, m, b):
            if b == 0:
                pe.wait_ge(x1_ready, m * PIECES + PIECES)
            else:
                pe.wait_ge(added, m * (UNITS * B) + 1)
            for k in range(KC):
                last = nc.tensor.transpose(db[b][:, k * P:(k + 1) * P], x1[:, k, b * TB:(b + 1) * TB], ident[:, :])
            last.then_inc(x1_rows, 1)

        def pe_logits(pe, m, b):
            o = rbk[:, b * E:(b + 1) * E]
            for k in range(KC):
                for q, u in THREE:
                    nc.tensor.matmul(o, x1p[:, u, k, b * TB:(b + 1) * TB], rwp[:, q, k, :],
                                     start=(k == 0 and q + u == 0), stop=False)
            for q in range(2):
                last = nc.tensor.matmul(o, ones[0:1, :], trp[0:1, q, b * E:(b + 1) * E], start=False, stop=(q == 1))
            last.then_inc(logits, 1)

        def half_ups(pe, m, h, todo):
            per = KC * len(THREE)
            for n in todo:
                j, r = divmod(n, 2 * per)
                w, r = divmod(r, per)
                k, t = divmod(r, len(THREE))
                if w == 0 and r == 0:
                    pe.wait_ge(s13_in[j % 2], (m * (HALVES * JC // 2) + (h * JC + j) // 2 + 1) * 16)
                    if j >= 2:
                        pe.wait_ge(hid_ready, chunk_no(m, h, j - 2) + 1)
                if (h, j, w, r) == (0, 1, 1, 0):
                    pe.wait_ge(nlog_ready, m + 1)
                q, s = THREE[t]
                mm = nc.tensor.matmul(ub[2 * (j % 2) + w][:, 0:N], s13[:, j % 2, w, q, k, :], x1p[:, s, k, :],
                                      start=(r == 0), stop=(r == per - 1))
                if w == 1 and r == per - 1:
                    mm.then_inc(up_done, 1)

        def expert_ups(pe, e, todo):
            per = KC * len(THREE)
            for n in todo:
                j, r = divmod(n, per)
                k, t = divmod(r, len(THREE))
                q, s = THREE[t]
                mm = nc.tensor.matmul(ub[j][:, 0:N], we1[:, ds(e * (2 * PART) + (q * PART + k * C + j * P), P)],
                                      x1p[:, s, k, :], start=(r == 0), stop=(r == per - 1))
                if r == per - 1:
                    mm.then_inc(up_done, 1)

        def downs(pe, m, w, weights, order, todo, first_unit=False):
            for n in todo:
                b, k = order[n // len(THREE)]
                q, s = THREE[n % len(THREE)]
                first, lastk = k == 0 and n % len(THREE) == 0, k == JC - 1 and n % len(THREE) == 2
                if first:
                    if first_unit:
                        pe.wait_ge(acc_set, m * B + (b + 1))
                    else:
                        pe.wait_ge(added, unit_no(m, w) * B + (b + 2 - B))
                if n % len(THREE) == 0:
                    pe.wait_ge(hid_ready, chunk_no(m, w, k) + 1)
                mm = nc.tensor.matmul(db[b][:, :], hid[:, k, s, b * TB:(b + 1) * TB], weights(q, k),
                                      start=first, stop=lastk)
                if lastk:
                    mm.then_inc(down_done, 1)

        H_ORDER = [(0, 0), (0, 1), (0, 2), (1, 0), (0, 3), (1, 1), (1, 2), (1, 3)]
        E_ORDER = [(b, k) for b in range(B) for k in range(JC)]
        DOWNS = B * JC * len(THREE)

        ROWS_STEP = {(0, 0): 0, (0, 6): 1}
        LOGITS_STEP = {(0, 2): 0, (0, 3): 1}

        def pe_half(pe, m, h, step0, rnn=True):
            nup = len(UPS[h])
            for s in range(HSTEPS[h]):
                if rnn:
                    pe_step(pe, step0 + s, (H0[h] + s) % 2)
                if (h, s) in ROWS_STEP:
                    pe_rows(pe, m, ROWS_STEP[h, s])
                if (h, s) == (0, 1):
                    pe.wait_ge(x1p_ready, (m + 1) * X1P)
                if (h, s) in LOGITS_STEP:
                    pe_logits(pe, m, LOGITS_STEP[h, s])
                if s < nup:
                    half_ups(pe, m, h, range(UPS[h][s - 1] if s else 0, UPS[h][s]))
                else:
                    r = HSTEPS[h] - nup
                    if s == nup:
                        pe.wait_ge(s2_in, (m * HALVES + h + 1) * 16)
                    downs(pe, m, h, lambda q, k: s2[:, q * PART + k * C:q * PART + (k + 1) * C], H_ORDER,
                          range((s - nup) * DOWNS // r, (s - nup + 1) * DOWNS // r), first_unit=(h == 0))

        def pe_expert(pe, m, e, step0, rnn=True):
            ups = JC * KC * len(THREE)
            for s in range(ESTEPS):
                if rnn:
                    pe_step(pe, step0 + s, s % 2)
                if s < UP_E:
                    expert_ups(pe, e, range(s * ups // UP_E, (s + 1) * ups // UP_E))
                else:
                    r = ESTEPS - UP_E
                    downs(pe, m, e + HALVES,
                          lambda q, k: we2[:, ds(e * (2 * PART) + (q * PART + k * C), C)], E_ORDER,
                          range((s - UP_E) * DOWNS // r, (s - UP_E + 1) * DOWNS // r))

        @block.tensor
        def _(pe):
            pe.wait_ge(consts, E + 4)
            pe.wait_ge(small_in, 16 * (4 + B))
            for b in range(B):
                for k in range(KC):
                    last = nc.tensor.matmul(rbk[0:1, b * E:(b + 1) * E], ct[:, k, b, :], rw[:, KC + k, :],
                                            start=(k == 0), stop=(k == KC - 1))
            last.then_inc(t_ps, 1)
            pe.wait_ge(t_row, 1)
            for c in range(2):
                pe_inputs(pe, 0, c)
            pe.wait_ge(w_split, 1)
            pe_xw(pe, 0, range(XW_ALL))
            pe.wait_ge(w_split, 2)
            pe.wait_ge(seeded, 2)
            with pe.Fori(0, NB - 1) as g:
                for s in range(XS):
                    pe_step(pe, g * XS + s, s % 2)
                    pe_ahead(pe, g + 1, s)
            for s in range(TB - (NB - 1) * XS):
                pe_step(pe, (NB - 1) * XS + s, s % 2)
            pe.wait_ge(rw_split, 2)
            with pe.Fori(1, NB) as i:
                for h in range(HALVES):
                    pe_half(pe, i - 1, h, i * TB + H0[h])
                with pe.Fori(0, E) as e:
                    pe_expert(pe, i - 1, e, i * TB + e * ESTEPS + H0[HALVES])
            for h in range(HALVES):
                pe_half(pe, NB - 1, h, 0, rnn=False)
            with pe.Fori(0, E) as e:
                pe_expert(pe, NB - 1, e, 0, rnn=False)

        def act_step(act, n, t, par):
            act.wait_ge(pre_ready, n + 1)
            nc.scalar.activation(hp[:, :, 0, :, :], pre[:, :, :, :], ACT.Tanh, scale=1.0 / WS).then_inc(h_hi, 1)
            nc.scalar.activation(hist[:, :, :, ds(t, 1)], pre[:, :, :, :], ACT.Tanh, scale=1.0 / WS)\
              .then_inc(h_kept, 1)
            act_seed(xw[:, :, :, ds(t, 1)], par)

        def act_seed(src, par):
            nc.scalar.activation(z[par][:, :, 2, :], src.rearrange("p j b o -> p j (b o)"), ACT.Copy)\
              .then_inc(seeded, 1)

        def act_xt(act, i, c, dst):
            act.wait_ge(xt_ps, i * 2 + (c + 1))
            nc.scalar.activation(dst[:, 2 * c:2 * c + 2, :].rearrange("p k n -> p (k n)"), db[c][:, :], ACT.Copy)\
              .then_inc(xt_ready, 1)

        def act_xp(act, i, c, src):
            act.wait_ge(xt_ready, i * 2 + (c + 1))
            nc.scalar.activation(xp[:, 0, 2 * c:2 * c + 2, :], src[:, 2 * c:2 * c + 2, :], ACT.Copy)\
              .then_inc(xp_hi, 1)

        def act_xw(act, i, j, t0, dst):
            act.wait_ge(xw_ps, i * KC + (j + 1))
            nc.scalar.activation(dst, ub[j][:, 0:N].rearrange("p (b t) -> p b t", b=B)[:, :, t0:],
                                 ACT.Identity, bias=b64[:, j:j + 1]).then_inc(xw_ready, 1)

        def act_ahead(act, i, s):
            if s == 0:
                if not (isinstance(i, int) and i == 1):
                    act.wait_ge(xt_out, (i - 1) * 16)
                act_xt(act, i, 0, x1)
            if s == 1:
                act_xp(act, i, 0, x1)
            if s == 2:
                act_xt(act, i, 1, x1)
            if s == 3:
                act_xp(act, i, 1, x1)
            if s == XS - 1:
                if not (isinstance(i, int) and i == 1):
                    act.wait_ge(acc_free, (i - 1) * 16)
                for j in range(KC):
                    act_xw(act, i, j, 0, acc[:, :, :].rearrange("p b c -> p (b c)")[:, j * N:(j + 1) * N]
                           .rearrange("p (b t) -> p b t", b=B))

        def act_x1p(act, m, c):
            g, t = x1_piece(c)
            act.wait_ge(x1_ready, m * PIECES + (PIECES if c == 2 else PIECES - 1))
            nc.scalar.activation(x1p[:, 0, :, :].rearrange("p k (b t) -> p (k b) t", b=B)[:, g, t],
                                 x1[:, :, :].rearrange("p k (b t) -> p (k b) t", b=B)[:, g, t], ACT.Copy)\
              .then_inc(x1_hi, 1)

        def act_acc(act, m, b):
            act.wait_ge(acc_free, (m + (NB - 1)) * 16)
            act.wait_ge(x1_rows, m * B + (b + 1))
            nc.scalar.activation(acc[:, b, :], db[b][:, :], ACT.Copy).then_inc(acc_set, 1)

        def act_gate(act, m, w, j, bank_no, func, scale):
            act.wait_ge(up_done, chunk_no(m, w, j) + 1)
            nc.scalar.activation(et[:, j % 2, :], ub[bank_no][:, 0:N], func, scale=scale).then_inc(act_done, 1)

        def act_hi(act, m, w, j, g, scale, done):
            act.wait_ge(done, (m * (HALVES * JC) + w * JC + j if done is g_done else chunk_no(m, w, j)) + 1)
            nc.scalar.activation(hid[:, j, 0, :], g[:, j % 2, :], ACT.Copy, scale=scale).then_inc(hid_hi, 1)

        H_GATE = [{4: 0, 7: 1, 10: 2, 12: 3}, {3: 0, 5: 1, 8: 2, 10: 3}]
        E_GATE = {2: 0, 3: 1, 5: 2, 6: 3}

        def act_half(act, m, h, step0, t0, rnn=True):
            if h == 0:
                act_x1p(act, m, 2)
            for s in range(HSTEPS[h]):
                if rnn:
                    act_step(act, step0 + s, t0 + s, (t0 + s) % 2)
                if (h, s) == (0, 4):
                    act.wait_ge(logits, (m + 1) * B)
                    nc.scalar.activation(nlog[:, :], rbk[:, 0:B * E], ACT.Copy, scale=-1.0 / WS)\
                      .then_inc(nlog_ready, 1)
                    act_acc(act, m, 0)
                if (h, s) == (0, 8):
                    act_acc(act, m, 1)
                if s in H_GATE[h]:
                    act_gate(act, m, h, H_GATE[h][s], 2 * (H_GATE[h][s] % 2), ACT.Tanh, 0.5 / WS)
                if s - 1 in H_GATE[h]:
                    act_hi(act, m, h, H_GATE[h][s - 1], gt, 1.0, g_done)

        def act_expert(act, m, e, step0, t0, rnn=True, last=False):
            for s in range(ESTEPS):
                if rnn:
                    act_step(act, step0 + s, t0 + s, s % 2)
                if s - 1 in E_GATE:
                    act_hi(act, m, e + HALVES, E_GATE[s - 1], et, GS, act_done)
                if s in E_GATE:
                    if E_GATE[s] >= 2:
                        act.wait_ge(hid_ready, chunk_no(m, e + HALVES, E_GATE[s] - 2) + 1)
                    act_gate(act, m, e + HALVES, E_GATE[s], E_GATE[s], ACT.Gelu, 1.0 / WS)
                if last and s in (7, 8):
                    act_x1p(act, m + 1, s - 7)

        def split_hi(act, dst, src):
            nc.scalar.activation(dst, src, ACT.Copy, scale=WS).then_inc(w_hi, 1)

        @block.scalar
        def _(act):
            n = PART // SL
            act.wait_ge(consts, E + 4)
            act.wait_ge(small_in, 16 * (4 + B))
            nc.scalar.activation(hp[:, :, 0, :, :], ct[:, :, :, :], ACT.Gelu).then_inc(h0_hi, 1)
            act.wait_ge(h0_hi, 1)
            nc.scalar.activation(hp[:, :, 0, :, :], ct[:, :, :, :], ACT.Copy).then_inc(h_hi, 1)
            act.wait_ge(t_ps, 1)
            nc.scalar.activation(trow[0:1, :], rbk[0:1, 0:B * E], ACT.Copy, scale=WS).then_inc(t_row, 1)
            act.wait_ge(t_row, 1)
            nc.scalar.activation(trp[0:1, 0, :], trow[0:1, :], ACT.Copy).then_inc(rw_hi, 1)
            nc.scalar.activation(rwp[:, 0, :, :], rw[:, 0:KC, :], ACT.Copy, scale=WS).then_inc(rw_hi, 1)
            for c in range(2):
                act_xt(act, 0, c, xt)
            for c in range(2):
                act_xp(act, 0, c, xt)
            act.wait_ge(xt_ready, 2)
            nc.scalar.activation(nlog[:, 0:1], ct[:, 0, 0, :], ACT.Copy).then_inc(xt_in, 16)
            for g, w in enumerate((wx, wh)):
                act.wait_ge(wxh_in[g], 16)
                nc.scalar.activation(w[:, 0:PART], stage[:, g, :], ACT.Copy, scale=WS).then_inc(w_hi, 1)
            act.wait_ge(b_scaled, 1)
            for j in range(KC):
                act.wait_ge(xw_ps, j + 1)
                nc.scalar.activation(xw0[:, j, :, :], ub[j][:, 0:N].rearrange("p (b t) -> p b t", b=B)[:, :, 0:2],
                                     ACT.Identity, bias=b64[:, j:j + 1]).then_inc(xw0_ready, 1)
                act_xw(act, 0, j, 2, xw[:, j, :, 0:TB - 2])
            act.wait_ge(xw0_ready, KC)
            for t in range(2):
                act_seed(xw0[:, :, :, t:t + 1], t)
            act.wait_ge(xw_ready, KC)
            for u in range(NSH // 2):
                for s in range(XS):
                    c, r = divmod(s, SL)
                    g = 2 * u + c
                    act_step(act, u * XS + s, u * XS + s, s % 2)
                    if r == 0:
                        act.wait_ge(staged[c], 16 * (u + 1))
                    o = (2 + g) * 2 * PART + r * n
                    split_hi(act, we2[:, o:o + n], stage[:, c, r * n:(r + 1) * n])
                    act_ahead(act, u + 1, s)

            def experts(e0, e1):
                with act.Fori(e0, e1) as e:
                    for s in range(XS):
                        c, r = divmod(s, SL)
                        t = e * XS + (NSH * SL + s)
                        act_step(act, t, t, s % 2)
                        if r == 0:
                            act.wait_ge(staged[c], e * 16 + 16 * (NSH // 2 + 1))
                            if e0 >= 2 and c == 1:
                                act.wait_ge(scratch_out, 16 * (2 * HALVES * JC + HALVES))
                        split_hi(act, (we1, we2)[c][:, ds(e * (2 * PART) + r * n, n)],
                                 stage[:, c, r * n:(r + 1) * n])
                        act_ahead(act, e + (NSH // 2 + 1), s)

            experts(0, 2)
            experts(2, E)
            with act.Fori(NSH // 2 + E, NB - 1) as u:
                for s in range(XS):
                    act_step(act, u * XS + s, u * XS + s, s % 2)
                    act_ahead(act, u + 1, s)
            act.wait_ge(tail_in, 16)
            for t in range((NB - 1) * XS, TB):
                act_step(act, t, t, t % 2)
                if t >= TB - 3 and t < TB - 1:
                    act_x1p(act, 0, t - (TB - 3))
            with act.Fori(1, NB) as i:
                act.wait_ge(xw_in[0], i * 16)
                for h in range(HALVES):
                    act_half(act, i - 1, h, i * TB + H0[h], H0[h])
                act.wait_ge(xw_in[1], i * 16)
                with act.Fori(0, E - 1) as e:
                    act_expert(act, i - 1, e, i * TB + e * ESTEPS + H0[HALVES], e * ESTEPS + H0[HALVES])
                act_expert(act, i - 1, E - 1, i * TB + TC, TC, last=True)
            for h in range(HALVES):
                act_half(act, NB - 1, h, 0, 0, rnn=False)
            with act.Fori(0, E) as e:
                act_expert(act, NB - 1, e, 0, 0, rnn=False)

        def dve_step(dve, n, t, par):
            dve.wait_ge(z_ready, n + 1)
            nc.vector.tensor_reduce(pre[:, :, :, 0], z[par].rearrange("p j c b -> p j b c"), axis=AX.X, op=ALU.add)\
              .then_inc(pre_ready, 1)
            dve.wait_ge(h_hi, n + 2)
            dve.wait_ge(h_kept, n + 1)
            nc.vector.tensor_tensor(hp[:, :, 1, :, :], hist[:, :, :, ds(t, 1)], hp[:, :, 0, :, :], ALU.subtract)\
              .then_inc(h_ready, 1)

        GATE_AT = (0, 5, 9, 13, 17, 22, 26)
        CHAIN = GATE_AT[-1]

        GATE_STEP = {(0, 9): 0, (0, 14): 1, (0, 15): 2, (1, 0): 3, (1, 1): 4, (1, 2): 5}

        def dve_gates(dve, m, stage_no):
            count = [GATE_AT[stage_no]]

            def link(ins):
                count[0] += 1
                ins.then_inc(chain, 1)
                dve.wait_ge(chain, m * CHAIN + count[0])

            def is_max():
                link(nc.vector.tensor_reduce(mx[:, :, 0], sel[:, :, :], axis=AX.X, op=ALU.max))
                link(nc.vector.tensor_tensor(m1[:, :, :], sel[:, :, :], mx[:, :, :].to_broadcast([P, B, E]),
                                             ALU.is_ge))

            def lowest(onehot):
                link(nc.vector.tensor_tensor(m1[:, :, :], m1[:, :, :], rev[:, :, :], ALU.mult))
                link(nc.vector.tensor_reduce(mx[:, :, 0], m1[:, :, :], axis=AX.X, op=ALU.max))
                link(nc.vector.tensor_tensor(onehot[:, :, :], m1[:, :, :], mx[:, :, :].to_broadcast([P, B, E]),
                                             ALU.is_equal))

            if stage_no == 0:
                dve.wait_ge(pow_ready, m + 1)
                link(nc.vector.tensor_scalar(pw[:, :], pw[:, :], 1.0, None, ALU.add))
                link(nc.vector.reciprocal(sg[:, :, :].rearrange("p b e -> p (b e)"), pw[:, :]))
                link(nc.vector.tensor_tensor(sel[:, :, :], sg[:, :, :], rb[:, :, :], ALU.add))
                is_max()
            if stage_no == 1:
                lowest(oh1)
                link(nc.vector.scalar_tensor_tensor(out=sel[:, :, :], in0=oh1[:, :, :], scalar=-BIG,
                                                    in1=sel[:, :, :], op0=ALU.mult, op1=ALU.add))
            if stage_no == 2:
                is_max()
                link(nc.vector.tensor_tensor(m1[:, :, :], m1[:, :, :], rev[:, :, :], ALU.mult))
                link(nc.vector.tensor_reduce(mx[:, :, 0], m1[:, :, :], axis=AX.X, op=ALU.max))
            if stage_no == 3:
                link(nc.vector.tensor_tensor(oh2[:, :, :], m1[:, :, :], mx[:, :, :].to_broadcast([P, B, E]),
                                             ALU.is_equal))
                link(nc.vector.tensor_tensor(m1[:, :, :], oh1[:, :, :], oh2[:, :, :], ALU.add))
                link(nc.vector.tensor_tensor(oh1[:, :, :], m1[:, :, :], sg[:, :, :], ALU.mult))
                link(nc.vector.tensor_reduce(den[:, :, 0], oh1[:, :, :], axis=AX.X, op=ALU.add))
            if stage_no == 4:
                link(nc.vector.tensor_scalar(okd[:, :, :], den[:, :, :], 1e-9, OS, ALU.is_gt, ALU.mult))
                link(nc.vector.tensor_scalar(alt[:, :, :], okd[:, :, :], -0.5, 0.5 * OS, ALU.mult, ALU.add))
                link(nc.vector.tensor_scalar(den[:, :, :], den[:, :, :], 1e-9, None, ALU.add))
                link(nc.vector.reciprocal(den[:, :, :], den[:, :, :]))
                link(nc.vector.tensor_tensor(den[:, :, :], den[:, :, :], okd[:, :, :], ALU.mult))
            if stage_no == 5:
                for b in range(B):
                    link(nc.vector.tensor_scalar(oh2[:, b, :], m1[:, b, :], alt[:, b, :], None, ALU.mult))
                for b in range(B):
                    link(nc.vector.scalar_tensor_tensor(out=gates[:, b * (1 + E) + 1:(b + 1) * (1 + E)], in0=oh1[:, b, :],
                                                        scalar=den[:, b, :], in1=oh2[:, b, :],
                                                        op0=ALU.mult, op1=ALU.add))
            assert count[0] == GATE_AT[stage_no + 1]

        def dve_silu(dve, m, h, j):
            a, b = ub[2 * (j % 2)][:, 0:N], ub[2 * (j % 2) + 1][:, 0:N]
            dve.wait_ge(act_done, chunk_no(m, h, j) + 1)
            nc.vector.scalar_tensor_tensor(out=ut[:, :], in0=et[:, j % 2, :], scalar=1.0, in1=a,
                                           op0=ALU.add, op1=ALU.mult).then_inc(u_done, 1)
            dve.wait_ge(u_done, m * (HALVES * JC) + (h * JC + j + 1))
            nc.vector.scalar_tensor_tensor(out=gt[:, j % 2, :], in0=ut[:, :], scalar=GS / (2.0 * WS * WS), in1=b,
                                           op0=ALU.mult, op1=ALU.mult).then_inc(g_done, 1)

        def dve_lo(dve, m, w, j, g, scale):
            dve.wait_ge(hid_hi, chunk_no(m, w, j) + 1)
            nc.vector.scalar_tensor_tensor(out=hid[:, j, 1, :], in0=g[:, j % 2, :], scalar=scale,
                                           in1=hid[:, j, 0, :], op0=ALU.mult, op1=ALU.subtract)\
               .then_inc(hid_ready, 1)

        def dve_add(dve, m, w, b, scalar):
            dve.wait_ge(added, unit_no(m, w) * B + (b + 1))
            dve.wait_ge(down_done, unit_no(m, w) * B + (b + 1))
            nc.vector.scalar_tensor_tensor(out=acc[:, b, :], in0=db[b][:, :], scalar=scalar, in1=acc[:, b, :],
                                           op0=ALU.mult, op1=ALU.add).then_inc(added, 1)

        def dve_half(dve, m, h, step0, t0, rnn=True):
            for s in range(HSTEPS[h]):
                if rnn:
                    dve_step(dve, step0 + s, t0 + s, (t0 + s) % 2)
                if (h, s) in GATE_STEP:
                    dve_gates(dve, m, GATE_STEP[h, s])
                if s in H_GATE[h]:
                    dve_silu(dve, m, h, H_GATE[h][s])
                if s - 1 in H_GATE[h]:
                    dve_lo(dve, m, h, H_GATE[h][s - 1], gt, 1.0)
                if s == HSTEPS[h] - 1:
                    if h == 0:
                        dve.wait_ge(acc_set, (m + 1) * B)
                    dve_add(dve, m, h, 0, OS)
                if s == 0 and h > 0:
                    dve_add(dve, m, h - 1, 1, OS)

        def dve_expert(dve, m, e, step0, t0, rnn=True):
            for s in range(ESTEPS):
                if rnn:
                    dve_step(dve, step0 + s, t0 + s, s % 2)
                if s - 1 in E_GATE:
                    dve_lo(dve, m, e + HALVES, E_GATE[s - 1], et, GS)
                if s == 0:
                    dve_add(dve, m, e + (HALVES - 1), 1, gates[:, ds(e + (1 + E), 1)])
                if s == UP_E + 3:
                    dve_add(dve, m, e + HALVES, 0, gates[:, ds(e + 1, 1)])

        def split_lo(dve, count, dst, hi, src):
            dve.wait_ge(w_hi, count)
            nc.vector.scalar_tensor_tensor(out=dst, in0=src, scalar=WS, in1=hi, op0=ALU.mult, op1=ALU.subtract)\
              .then_inc(w_split, 1)

        @block.vector
        def _(dve):
            n = PART // SL
            dve.wait_ge(consts, E + 4)
            dve.wait_ge(small_in, 16 * (4 + B))
            nc.vector.tensor_scalar(b64[:, :], b64[:, :], WS, None, ALU.mult).then_inc(b_scaled, 1)
            nc.vector.memset(gates[:, :], OS).then_inc(added, 1)
            dve.wait_ge(h_hi, 1)
            nc.vector.tensor_tensor(hp[:, :, 1, :, :], ct[:, :, :, :], hp[:, :, 0, :, :], ALU.subtract)\
              .then_inc(h_ready, 1)
            dve.wait_ge(rw_hi, 1)
            nc.vector.tensor_tensor(trp[0:1, 1, :], trow[0:1, :], trp[0:1, 0, :], ALU.subtract).then_inc(rw_split, 1)
            dve.wait_ge(rw_hi, 2)
            nc.vector.scalar_tensor_tensor(out=rwp[:, 1, :, :], in0=rw[:, 0:KC, :], scalar=WS, in1=rwp[:, 0, :, :],
                                           op0=ALU.mult, op1=ALU.subtract).then_inc(rw_split, 1)
            for g, w in enumerate((wx, wh)):
                if g == 0:
                    for c in range(2):
                        k = slice(2 * c, 2 * c + 2)
                        dve.wait_ge(xp_hi, c + 1)
                        nc.vector.tensor_tensor(xp[:, 1, k, :], xt[:, k, :], xp[:, 0, k, :], ALU.subtract)\
                          .then_inc(xp_ready, 1)
                split_lo(dve, g + 1, w[:, PART:2 * PART], w[:, 0:PART], stage[:, g, :])
            for g in range(NSH):
                for s in range(SL):
                    dve_step(dve, g * SL + s, g * SL + s, s % 2)
                    o = (2 + g) * 2 * PART + s * n
                    split_lo(dve, 2 + g * SL + s + 1, we2[:, PART + o:PART + o + n], we2[:, o:o + n],
                             stage[:, g % 2, s * n:(s + 1) * n])
            with dve.Fori(0, E) as e:
                for c, w in enumerate((we1, we2)):
                    for s in range(SL):
                        t = e * XS + (NSH * SL + c * SL + s)
                        dve_step(dve, t, t, s % 2)
                        split_lo(dve, t + 3, w[:, ds(e * (2 * PART) + (PART + s * n), n)],
                                 w[:, ds(e * (2 * PART) + s * n, n)], stage[:, c, s * n:(s + 1) * n])
            with dve.Fori((NSH + NEX), TB // SL) as g:
                for s in range(SL):
                    dve_step(dve, g * SL + s, g * SL + s, s % 2)
            with dve.Fori(1, NB) as i:
                for h in range(HALVES):
                    dve_half(dve, i - 1, h, i * TB + H0[h], H0[h])
                with dve.Fori(0, E) as e:
                    dve_expert(dve, i - 1, e, i * TB + e * ESTEPS + H0[HALVES],
                               e * ESTEPS + H0[HALVES])
                dve_add(dve, i - 1, UNITS - 1, 1, gates[:, B * (1 + E) - 1:B * (1 + E)])
            for h in range(HALVES):
                dve_half(dve, NB - 1, h, 0, 0, rnn=False)
            with dve.Fori(0, E) as e:
                dve_expert(dve, NB - 1, e, 0, 0, rnn=False)
            dve_add(dve, NB - 1, UNITS - 1, 1, gates[:, B * (1 + E) - 1:B * (1 + E)])


_INS = ["x", "cond_1024", "L0_cond_Wx", "L0_cond_Wh", "L0_cond_b", "L1_cond_router_W", "L1_cond_router_bias",
        "L1_cond_w1", "L1_cond_w3", "L1_cond_w2", "L1_cond_W1e", "L1_cond_W2e"]


def kernel(**inputs):
    import numpy as _np
    import concourse.bacc as _bacc
    from concourse import mybir as _mybir
    from concourse.bass_utils import run_bass_kernel_spmd as _run

    nc = _bacc.Bacc("TRN2", target_bir_lowering=False, num_devices=1)
    arrays, args = {}, []
    for name in _INS:
        a = _np.ascontiguousarray(inputs[name])
        arrays[f"in_{name}"] = a
        args.append(nc.dram_tensor(f"in_{name}", a.shape, _mybir.dt.from_np(a.dtype), kind="ExternalInput").ap())
    shape = inputs["x"].shape
    args.append(nc.dram_tensor("out_0", shape, _mybir.dt.float32, kind="ExternalOutput").ap())
    rnn_then_moe_kernel(nc, *args)
    r = _run(nc, [arrays], core_ids=[0])
    return r.results[0]["out_0"]
```

```python
import math

import concourse.bass as bass
from concourse import mybir
from contextlib import ExitStack


def rnn_then_moe_kernel(
    nc: bass.Bass,
    x: bass.AP,
    cond: bass.AP,
    Wx: bass.AP,
    Wh: bass.AP,
    b_rnn: bass.AP,
    router_W: bass.AP,
    router_bias: bass.AP,
    w1: bass.AP,
    w3: bass.AP,
    w2: bass.AP,
    W1e: bass.AP,
    W2e: bass.AP,
    out: bass.AP,
):
    f32 = mybir.dt.float32
    f16 = mybir.dt.float16
    ALU = mybir.AluOpType
    ACT = mybir.ActivationFunctionType
    AX = mybir.AxisListType
    ds = bass.ds

    P = 128
    B, T, C = x.shape
    E, _, HE = W1e.shape
    HS = w1.shape[1]
    TB = P
    NB = T // TB
    KC = C // P
    N = B * TB
    HALVES = HS // HE
    JC = HE // P
    UNITS = HALVES + E
    CH = UNITS * JC
    PART = KC * C
    WS = 64.0
    GS = 2.0 * WS
    OS = 1.0 / (3.0 * GS * WS)
    ESTEPS = 12
    H0 = [0, 17, TB - E * ESTEPS]
    HSTEPS = [H0[1] - H0[0], H0[2] - H0[1]]
    UPS = [[0, 11, 18, 24, 33, 42, 48, 58, 67, 77, 87, 96], [(s + 1) * 96 // 10 for s in range(10)]]
    UP_E = ESTEPS // 2
    NSH = 3 * HALVES
    BIG = 1.0e30
    XS = TB // NB
    THIRD = -(-PART // 3 // 64) * 64
    SPLIT_SHARED = [[(0, k * C, C)] for k in range(KC)] + [[(1, 0, C)], [(1, C, C)], [(1, 2 * C, C), (1, 3 * C, C)]]
    SPLIT_EXPERT = [[(0, k * C, C)] for k in range(KC)] + [[(1, 0, THIRD)], [(1, THIRD, THIRD)],
                                                           [(1, 2 * THIRD, PART - 2 * THIRD)]]
    S0 = 4
    SL = KC
    SE = SL + 3
    PIECES = HALVES + E
    TC = TB - ESTEPS
    LEAD = 2
    X1P = 3
    G = KC * B

    sc13 = nc.dram_tensor("shared_up_parts", [HALVES * JC, P, 2, 2, KC, P], f16).ap()
    xts = nc.dram_tensor("x_channels", [NB, P, KC * N], f32).ap()
    xws = nc.dram_tensor("xw_channels", [P, G, LEAD + T + 2], f32).ap()
    sc2 = nc.dram_tensor("shared_down_parts", [HALVES, P, 2 * PART], f16).ap()

    ctx = ExitStack()
    with ctx:
        def sb(name, shape, dt):
            return ctx.enter_context(nc.sbuf_tensor(name, shape, dt))

        def sem(name):
            return ctx.enter_context(nc.semaphore(name))

        wx = sb("wx", [P, 2 * PART], f16)
        wh = sb("wh", [P, 2 * PART], f16)
        we1 = sb("we1", [P, E * 2 * PART], f16)
        we2 = sb("we2", [P, E * 2 * PART], f16)
        stream = sb("stream", [P, 2 * PART], f32)
        s13 = stream[:, 0:PART].bitcast(f16).rearrange("p (s w q k c) -> p s w q k c", s=2, w=2, q=2, k=KC)
        s2 = stream[:, PART:2 * PART].bitcast(f16)
        stage = stream[:, :].rearrange("p (s n) -> p s n", s=2)
        hp = sb("hp", [P, KC, 2, B, 1], f16)
        hist = sb("hist", [P, KC, B, TB], f32)
        xw = sb("xw", [P, KC, B, TB], f32)
        xw0 = sb("xw0", [P, KC, B, 2], f32)
        pre = sb("pre", [P, KC, B, 1], f32)
        xn = sb("xn", [P, B, C], f32)
        xt = sb("xt", [P, KC, N], f32)
        xp = sb("xp", [P, 2, KC, N], f16)
        x1 = sb("x1", [P, KC, N], f32)
        x1p = sb("x1p", [P, 2, KC, N], f16)
        et = sb("et", [P, 2, N], f32)
        ut = sb("ut", [P, N], f32)
        gt = sb("gt", [P, 2, N], f32)
        hid = sb("hid", [P, JC, 2, N], f16)
        acc = sb("acc", [P, B, C], f32)
        pad = sb("pad", [P, G, 2], f32)
        ident = sb("ident", [P, P], f32)
        ones = sb("ones", [1, P], f16)
        ct = sb("ct", [P, KC, B, 1], f32)
        b64 = sb("b64", [P, KC], f32)
        rw = sb("rw", [P, 2 * KC, E], f32)
        rwp = sb("rwp", [P, 2, KC, E], f16)
        rb = sb("rb", [P, B, E], f32)
        rev = sb("rev", [P, B, E], f32)
        trow = sb("trow", [1, B * E], f32)
        trp = sb("trp", [1, 2, B * E], f16)
        base = sb("base", [P, B * E], f32)
        nlog = sb("nlog", [P, B * E], f32)
        pw = sb("pw", [P, B * E], f32)
        sg = sb("sg", [P, B, E], f32)
        sel = sb("sel", [P, B, E], f32)
        m1 = sb("m1", [P, B, E], f32)
        oh1 = sb("oh1", [P, B, E], f32)
        oh2 = sb("oh2", [P, B, E], f32)
        mx = sb("mx", [P, B, 1], f32)
        den = sb("den", [P, B, 1], f32)
        okd = sb("okd", [P, B, 1], f32)
        alt = sb("alt", [P, B, 1], f32)
        gates = sb("gates", [P, B * (1 + E)], f32)

        def bank(name):
            return ctx.enter_context(nc.psum_tensor(name, [P, 512], f32))

        zb = [bank(f"zb{i}") for i in range(2)]
        ub = [bank(f"ub{i}") for i in range(4)]
        db = [bank(f"db{i}") for i in range(2)]
        rbk = ub[3]
        z = [zb[i][:, 0:KC * 3 * B].rearrange("p (j c b) -> p j c b", j=KC, c=3) for i in range(2)]

        small_in = sem("small_in")
        x_in = [sem("x_in0"), sem("x_in1")]
        xw_in = [sem("xw_in0"), sem("xw_in1")]
        xt_in = sem("xt_in")
        tail_in = sem("tail_in")
        pad_out = sem("pad_out")
        xt_out = [sem("xt_out0"), sem("xt_out1")]
        wxh_in = [sem("wx_in0"), sem("wx_in1"), sem("wh_in0"), sem("wh_in1")]
        staged = [sem("staged0"), sem("staged1")]
        s13_in = [sem("s13_in0"), sem("s13_in1")]
        s2_in = sem("s2_in")
        scratch_out = [sem("up_parts_out"), sem("down_parts_out")]
        acc_free = sem("acc_free")
        consts = sem("consts")
        ident0 = sem("ident0")
        b_scaled = sem("b_scaled")
        table_set = sem("table_set")
        t_ps = sem("t_ps")
        t_row = sem("t_row")
        rw_hi = sem("rw_hi")
        rw_split = sem("rw_split")
        w_hi = sem("w_hi")
        w_split = sem("w_split")
        z_ready = sem("z_ready")
        seeded = sem("seeded")
        pre_ready = sem("pre_ready")
        h_kept = sem("h_kept")
        h_hi = sem("h_hi")
        h_ready = sem("h_ready")
        xt_ps = sem("xt_ps")
        xt_ready = sem("xt_ready")
        xp_hi = sem("xp_hi")
        xp_ready = sem("xp_ready")
        xp_used = sem("xp_used")
        xw_ps = sem("xw_ps")
        xw_ready = sem("xw_ready")
        xw0_ready = sem("xw0_ready")
        x1_ready = sem("x1_ready")
        x1_hi = sem("x1_hi")
        x1p_ready = sem("x1p_ready")
        x1_rows = sem("x1_rows")
        acc_set = sem("acc_set")
        logits = sem("logits")
        nlog_ready = sem("nlog_ready")
        pow_ready = sem("pow_ready")
        chain = sem("chain")
        up_done = sem("up_done")
        act_done = sem("act_done")
        u_done = sem("u_done")
        g_done = sem("g_done")
        hid_hi = sem("hid_hi")
        hid_ready = sem("hid_ready")
        down_done = sem("down_done")
        added = sem("added")

        block = ctx.enter_context(nc.Block())

        def chunk_no(m, w, j):
            return m * CH + w * JC + j

        def unit_no(m, w):
            return m * UNITS + w

        def peeled(i, *numbers):
            return isinstance(i, int) and i in numbers

        def to_scratch(sp, g):
            sp.wait_ge(w_split, S0 + SL * (g + 1))
            if g < 2 * HALVES:
                w, h = g // HALVES, g % HALVES
                sp.dma_start(sc13[h * JC:(h + 1) * JC, :, w, :, :, :].rearrange("j p q k c -> p j (q k c)"),
                             we2[:, (2 + g) * 2 * PART:(3 + g) * 2 * PART].rearrange("p (j n) -> p j n", j=JC))\
                  .then_inc(scratch_out[0], 16)
            else:
                sp.dma_start(sc2[g - 2 * HALVES, :, :], we2[:, (2 + g) * 2 * PART:(3 + g) * 2 * PART])\
                  .then_inc(scratch_out[1], 16)

        def x_load(sp, i, c):
            if not peeled(i, 0):
                sp.wait_ge(xt_ps, i * 2 + (c - 1))
            n = C // 2
            sp.dma_start(xn[:, :, c * n:(c + 1) * n], x[:, ds(i * TB, TB), c * n:(c + 1) * n]
                         .rearrange("b t c -> t b c")).then_inc(x_in[c], 16)

        def up_weights(sp, h, j):
            sp.dma_start(s13[:, j % 2, :, :, :, :].rearrange("p w q k c -> p (w q k c)"),
                         sc13[h * JC + j, :, :, :, :, :].rearrange("p w q k c -> p (w q k c)"))\
              .then_inc(s13_in[j % 2], 16)

        def down_weights(sp, h):
            sp.dma_start(s2, sc2[h, :, :]).then_inc(s2_in, 16)

        def first_weights(sp):
            for j in range(2):
                up_weights(sp, 0, j)
            down_weights(sp, 0)

        def weights(sp, m, last=False):
            for h in range(HALVES):
                for j in range(JC):
                    hn, jn = (h, j + 2) if j + 2 < JC else (h + 1, j + 2 - JC)
                    if hn == HALVES and last:
                        continue
                    sp.wait_ge(up_done, chunk_no(m, h, j) + 1)
                    up_weights(sp, hn % HALVES, jn)
                if h < HALVES - 1 or not last:
                    sp.wait_ge(down_done, (unit_no(m, h) + 1) * B)
                    down_weights(sp, (h + 1) % HALVES)

        def xw_half(sp, i, c):
            n = TB // 2
            sp.wait_ge(seeded, (i - 1) * TB + ((c + 1) * n + 2))
            sp.dma_start(xw[:, :, :, c * n:(c + 1) * n].rearrange("p k b t -> p (k b) t"),
                         xws[:, :, ds(i * TB + (LEAD + 2 + c * n), n)]).then_inc(xw_in[c], 16)

        def block_dma(sp, i, last=False):
            xw_half(sp, i, 1)
            sp.wait_ge(x1_ready, i * PIECES)
            sp.dma_start(xt[:, :, :].rearrange("p k n -> p (k n)"),
                         xts.rearrange("i p n -> (i p) n")[ds(i * P, P), :]).then_inc(xt_in, 16)
            weights(sp, i - 1)
            if not last:
                xw_half(sp, i + 1, 0)
            block_out(sp, i - 1)

        def block_out(sp, m):
            sp.wait_ge(added, (m + 1) * (UNITS * B) + 1)
            sp.dma_start(out[:, ds(m * TB, TB), :].rearrange("b t c -> t b c"), acc[:, :, :]).then_inc(acc_free, 16)

        def w0_slice(w, c, q=0):
            return w[:, q * PART + c * (PART // 2):q * PART + (c + 1) * (PART // 2)]

        def k_rows(w, r0, c0):
            return w[r0:r0 + C, c0:c0 + C].rearrange("(k p) n -> p k n", p=P)

        def stage_shared(sp, g):
            jobs = [k_rows(w, 0, h * HE) for w in (w1, w3) for h in range(HALVES)]
            jobs += [k_rows(w2, h * HE, 0) for h in range(HALVES)]
            sp.wait_ge(w_split, S0 + SL * (g - 1) if g >= 2 else S0 // 2 * (g + 1))
            sp.dma_start(stage[:, g % 2, :].rearrange("p (k n) -> p k n", k=KC), jobs[g]).then_inc(staged[g % 2], 16)

        def stage_expert(sp, e, c):
            if peeled(e, 0):
                sp.wait_ge(w_split, S0 + SL * (NSH - 1 + c))
            else:
                sp.wait_ge(w_split, e * SE + (S0 + SL * NSH + (SL - SE if c == 0 else 0)))
            sp.dma_start(stage[:, c, :].rearrange("p (k n) -> p k n", k=KC),
                         (W1e, W2e)[c].rearrange("e r n -> (e r) n")[ds(e * C, C), :]
                         .rearrange("(k p) n -> p k n", p=P)).then_inc(staged[c], 16)

        def store_x(sp, i, c):
            sp.wait_ge(xt_ready, i * 2 + (c + 1))
            sp.dma_start(xts.rearrange("i p n -> (i p) n")[ds(i * P, P), c * 2 * N:(c + 1) * 2 * N],
                         x1[:, 2 * c:2 * c + 2, :].rearrange("p k n -> p (k n)")).then_inc(xt_out[c], 16)

        def store_xw(sp, i):
            sp.wait_ge(xw_ready, i * KC + KC)
            sp.dma_start(xws[:, :, ds(i * TB + LEAD, TB)], acc[:, :, :].rearrange("p b c -> p (b c)")
                         .rearrange("p (g t) -> p g t", t=TB)).then_inc(acc_free, 16)

        @block.sync
        def _(sp):
            for c in range(2):
                x_load(sp, 0, c)
            with nc.allow_non_contiguous_dma(reason="a few KB of constants, once"):
                for b in range(B):
                    sp.dma_start(ct[:, :, b, 0], cond[b, :].rearrange("(k p) -> p k", p=P)).then_inc(small_in, 16)
                sp.dma_start(b64[:, :], b_rnn.rearrange("(k p) -> p k", p=P)).then_inc(small_in, 16)
                sp.dma_start(rw[:, :, :], router_W.rearrange("(k p) e -> p k e", p=P)).then_inc(small_in, 16)
                for b in range(B):
                    sp.dma_start(rb[:, b, :], router_bias.rearrange("(o e) -> o e", o=1).to_broadcast([P, E]))\
                      .then_inc(small_in, 16)
            for n in range(S0):
                g, c = n // 2, n % 2
                src = (Wx, Wh)[g][c * (C // 2):(c + 1) * (C // 2), :]
                sp.dma_start(w0_slice(stage[:, g, :], c).rearrange("p (k n) -> p k n", n=C),
                             src.rearrange("(k p) n -> p k n", p=P)).then_inc(wxh_in[n], 16)
            for c in range(2):
                x_load(sp, 1, c)
            stage_shared(sp, 0)
            stage_shared(sp, 1)
            def prepare(g, stage_next=None, scratch=((), ())):
                if not peeled(g, 0, 1):
                    store_xw(sp, g - 1)
                if not peeled(g, 0):
                    store_x(sp, g, 1)
                for c in range(2):
                    if not peeled(g, NB - 2, NB - 1):
                        x_load(sp, g + 2, c)
                    if stage_next is not None:
                        stage_next(c)
                    for n in scratch[c]:
                        to_scratch(sp, n)
                    if c == 0 and not peeled(g, NB - 1):
                        store_x(sp, g + 1, 0)

            def stage_job(n):
                if n < NSH:
                    stage_shared(sp, n)
                else:
                    stage_expert(sp, (n - NSH) // 2, n % 2)

            SCRATCH = [((), (0,)), ((), (1,)), ((), (2,)), ((), (3,)), ((), ()), ((4,), ()), ((5,), ())]
            for g in range(len(SCRATCH)):
                prepare(g, lambda c: stage_job(2 * g + 2 + c), SCRATCH[g])
            sp.wait_ge(consts, E + 4)
            sp.dma_start(xws[:, :, LEAD + T:LEAD + T + 2], pad[:, :, :]).then_inc(pad_out, 16)
            sp.wait_ge(acc_free, 16)
            sp.dma_start(xw[:, :, :, TB - 2:TB].rearrange("p k b t -> p (k b) t"), xws[:, :, LEAD + TB:LEAD + TB + 2])\
              .then_inc(tail_in, 16)
            with sp.Fori(len(SCRATCH), NSH // 2 + E - 1) as g:
                prepare(g, lambda c: stage_expert(sp, g - (NSH // 2 - 1), c))
            prepare(NSH // 2 + E - 1)
            sp.wait_ge(w_split, S0 + SL * NSH + SE * E)
            sp.wait_ge(scratch_out[0], 16 * 2 * HALVES)
            sp.wait_ge(scratch_out[1], 16 * HALVES)
            first_weights(sp)
            with sp.Fori(NSH // 2 + E, NB - 2) as g:
                prepare(g)
            xw_half(sp, 1, 0)
            for g in range(NB - 2, NB):
                prepare(g)
            store_xw(sp, NB - 1)
            sp.wait_ge(acc_free, (NB - 1) * 16)
            for c in range(2):
                sp.wait_ge(xt_out[c], (NB - 1) * 16)
            sp.wait_ge(pad_out, 16)
            with sp.Fori(1, NB - 1) as i:
                block_dma(sp, i)
            block_dma(sp, NB - 1, last=True)
            weights(sp, NB - 1, last=True)
            block_out(sp, NB - 1)
            sp.wait_ge(acc_free, (2 * NB - 1) * 16)

        def pool_inputs(pool, i, src):
            for c in range(2):
                k = slice(2 * c, 2 * c + 2)
                pool.wait_ge(xp_hi, i * 2 + (c + 1))
                nc.gpsimd.tensor_tensor(xp[:, 1, k, :], src[:, k, :], xp[:, 0, k, :], ALU.subtract)\
                  .then_inc(xp_ready, 1)

        def pool_x1(pool, m, t0, n, pieces=1):
            pool.wait_ge(h_kept, m * TB + t0 + n)
            nc.gpsimd.tensor_tensor(x1[:, :, :].rearrange("p k (b t) -> p (k b) t", b=B)[:, :, ds(t0, n)],
                                    xt[:, :, :].rearrange("p k (b t) -> p (k b) t", b=B)[:, :, ds(t0, n)],
                                    hist[:, :, :, :].rearrange("p k b t -> p (k b) t")[:, :, ds(t0, n)],
                                    ALU.add).then_inc(x1_ready, pieces)

        def pool_block(pool, m):
            if peeled(m, 0):
                pool.wait_ge(xt_ready, 2)
                pool_x1(pool, m, 0, TC, PIECES - 1)
            else:
                pool.wait_ge(xt_in, m * 16)
                for h in range(HALVES):
                    pool_x1(pool, m, H0[h], HSTEPS[h])
                with pool.Fori(0, E - 1) as e:
                    pool_x1(pool, m, e * ESTEPS + H0[HALVES], ESTEPS)
            for c in range(2):
                pool_x1p(pool, m, c)
            pool_x1(pool, m, TC, ESTEPS)
            pool_x1p(pool, m, 2)

        def x1_piece(c):
            return [(slice(0, KC), slice(0, TC)), (slice(KC, 2 * KC), slice(0, TC)), (slice(0, G), slice(TC, TB))][c]

        def pool_x1p(pool, m, c):
            g, t = x1_piece(c)
            pool.wait_ge(x1_hi, m * X1P + (c + 1))
            nc.gpsimd.tensor_tensor(x1p[:, 1, :, :].rearrange("p k (b t) -> p (k b) t", b=B)[:, g, t],
                                    x1[:, :, :].rearrange("p k (b t) -> p (k b) t", b=B)[:, g, t],
                                    x1p[:, 0, :, :].rearrange("p k (b t) -> p (k b) t", b=B)[:, g, t],
                                    ALU.subtract).then_inc(x1p_ready, 1)

        def pool_pow(pool, m):
            pool.wait_ge(nlog_ready, m + 1)
            nc.gpsimd.tensor_tensor(pw[:, :], base[:, :], nlog[:, :], ALU.pow).then_inc(pow_ready, 1)

        @block.gpsimd
        def _(pool):
            nc.gpsimd.memset(ones[:, :], 1.0).then_inc(consts, 1)
            nc.gpsimd.memset(pad[:, :, :], 0.0).then_inc(consts, 1)
            nc.gpsimd.memset(base[:, :], math.e).then_inc(consts, 1)
            for e in range(E):
                nc.gpsimd.memset(rev[:, :, e], float(E - e)).then_inc(consts, 1)
            nc.gpsimd.memset(ident[:, :], 0.0).then_inc(ident0, 1)
            pool.wait_ge(ident0, 1)
            nc.gpsimd.affine_select(out=ident[:, :], in_=ident[:, :], compare_op=ALU.not_equal, fill=1.0, base=0,
                                    pattern=[[-1, P]], channel_multiplier=1).then_inc(consts, 1)
            pool_inputs(pool, 0, xt)
            with pool.Fori(1, NB) as i:
                pool_inputs(pool, i, x1)
            for c in range(2):
                pool.wait_ge(xt_out[c], (NB - 1) * 16)
            pool.wait_ge(xp_ready, NB * 2)
            pool_block(pool, 0)
            with pool.Fori(1, NB) as i:
                pool_pow(pool, i - 1)
                pool_block(pool, i)
            pool_pow(pool, NB - 1)

        THREE = ((0, 0), (0, 1), (1, 0))

        def wpart(w, q, k, c0, n):
            return w[:, q * PART + k * C + c0:q * PART + k * C + c0 + n]

        def pe_step(pe, n, par):
            pe.wait_ge(h_hi, n + 1)
            for j in range(KC):
                for k in range(KC):
                    nc.tensor.matmul(z[par][:, j, 0, :], wpart(wh, 1, k, j * P, P), hp[:, k, 0, :, 0],
                                     start=(j == 0 and k == 0), stop=False, skip_group_check=True)
            pe.wait_ge(h_ready, n + 1)
            for j in range(KC):
                for k in range(KC):
                    last = nc.tensor.matmul(z[par][:, j, 0:2, :], wpart(wh, 0, k, j * P, P), hp[:, k, :, :, 0],
                                            start=False, stop=(k == KC - 1), skip_group_check=True)
            last.then_inc(z_ready, 1)

        def pe_inputs(pe, i, todo):
            for n in todo:
                k, b = n // B, n % B
                c, r = divmod(n, 2 * B)
                if r == 0:
                    pe.wait_ge(x_in[c], (i + 1) * 16)
                    if not peeled(i, 0):
                        pe.wait_ge(xt_ready, i * 2 + (c - 1))
                tr = nc.tensor.transpose(db[c][:, r * TB:(r + 1) * TB], xn[:, b, k * P:(k + 1) * P], ident[:, :])
                if r == 2 * B - 1:
                    tr.then_inc(xt_ps, 1)

        XW_ALL = KC * KC * len(THREE)

        def pe_xw(pe, i, todo):
            for n in todo:
                c, r = divmod(n, XW_ALL // 2)
                j, r = divmod(r, 2 * len(THREE))
                k, t = 2 * c + r // len(THREE), r % len(THREE)
                q, u = THREE[t]
                if (c, r) == (0, 0) and not peeled(i, 0):
                    pe.wait_ge(xw_ready, i * KC + (j + 1 - KC))
                if (j, r) == (0, 0):
                    pe.wait_ge(xp_ready, i * 2 + (c + 1))
                mm = nc.tensor.matmul(ub[j][:, 0:N], wpart(wx, q, k, j * P, P), xp[:, u, k, :],
                                      start=(c == 0 and r == 0), stop=(c == 1 and r == 2 * len(THREE) - 1))
                if r == 2 * len(THREE) - 1:
                    if c == 1:
                        mm.then_inc(xw_ps, 1)
                    elif j == KC - 1:
                        mm.then_inc(xp_used, 1)

        TR = (0, 1, 2, 4, 4, 5, 6, 7, 8)

        def pe_ahead(pe, g, s):
            if not peeled(g, NB - 1):
                pe_inputs(pe, g + 1, range(TR[s], TR[s + 1]))
            if not peeled(g, 0):
                pe_xw(pe, g, range(s * XW_ALL // XS, (s + 1) * XW_ALL // XS))

        def pe_rows(pe, m, b):
            if b == 0:
                pe.wait_ge(x1_ready, m * PIECES + PIECES)
            else:
                pe.wait_ge(added, m * (UNITS * B) + 1)
            for k in range(KC):
                last = nc.tensor.transpose(db[b][:, k * P:(k + 1) * P], x1[:, k, b * TB:(b + 1) * TB], ident[:, :])
            last.then_inc(x1_rows, 1)

        def pe_logits(pe, m, b):
            o = rbk[:, b * E:(b + 1) * E]
            for k in range(KC):
                for q, u in THREE:
                    nc.tensor.matmul(o, x1p[:, u, k, b * TB:(b + 1) * TB], rwp[:, q, k, :],
                                     start=(k == 0 and q + u == 0), stop=False)
            for q in range(2):
                last = nc.tensor.matmul(o, ones[0:1, :], trp[0:1, q, b * E:(b + 1) * E], start=False, stop=(q == 1))
            last.then_inc(logits, 1)

        def half_ups(pe, m, h, todo):
            per = KC * len(THREE)
            for n in todo:
                j, r = divmod(n, 2 * per)
                w, r = divmod(r, per)
                k, t = divmod(r, len(THREE))
                if w == 0 and r == 0:
                    pe.wait_ge(s13_in[j % 2], (m * (HALVES * JC // 2) + (h * JC + j) // 2 + 1) * 16)
                    if j >= 2:
                        pe.wait_ge(hid_ready, chunk_no(m, h, j - 2) + 1)
                if (h, j, w, r) == (0, 1, 1, 0):
                    pe.wait_ge(nlog_ready, m + 1)
                q, s = THREE[t]
                mm = nc.tensor.matmul(ub[2 * (j % 2) + w][:, 0:N], s13[:, j % 2, w, q, k, :], x1p[:, s, k, :],
                                      start=(r == 0), stop=(r == per - 1))
                if w == 1 and r == per - 1:
                    mm.then_inc(up_done, 1)

        def expert_ups(pe, e, todo):
            per = KC * len(THREE)
            for n in todo:
                j, r = divmod(n, per)
                k, t = divmod(r, len(THREE))
                q, s = THREE[t]
                mm = nc.tensor.matmul(ub[j][:, 0:N], we1[:, ds(e * (2 * PART) + (q * PART + k * C + j * P), P)],
                                      x1p[:, s, k, :], start=(r == 0), stop=(r == per - 1))
                if r == per - 1:
                    mm.then_inc(up_done, 1)

        def downs(pe, m, w, weights, order, todo, first_unit=False):
            for n in todo:
                b, k = order[n // len(THREE)]
                q, s = THREE[n % len(THREE)]
                first, lastk = k == 0 and n % len(THREE) == 0, k == JC - 1 and n % len(THREE) == 2
                if first:
                    if first_unit:
                        pe.wait_ge(acc_set, m * B + (b + 1))
                    else:
                        pe.wait_ge(added, unit_no(m, w) * B + (b + 2 - B))
                if n % len(THREE) == 0:
                    pe.wait_ge(hid_ready, chunk_no(m, w, k) + 1)
                mm = nc.tensor.matmul(db[b][:, :], hid[:, k, s, b * TB:(b + 1) * TB], weights(q, k),
                                      start=first, stop=lastk)
                if lastk:
                    mm.then_inc(down_done, 1)

        H_ORDER = [(0, 0), (0, 1), (0, 2), (1, 0), (0, 3), (1, 1), (1, 2), (1, 3)]
        E_ORDER = [(b, k) for b in range(B) for k in range(JC)]
        DOWNS = B * JC * len(THREE)

        ROWS_STEP = {(0, 0): 0, (0, 6): 1}
        LOGITS_STEP = {(0, 2): 0, (0, 3): 1}

        def pe_half(pe, m, h, step0, rnn=True):
            nup = len(UPS[h])
            for s in range(HSTEPS[h]):
                if rnn:
                    pe_step(pe, step0 + s, (H0[h] + s) % 2)
                if (h, s) in ROWS_STEP:
                    pe_rows(pe, m, ROWS_STEP[h, s])
                if (h, s) == (0, 1):
                    pe.wait_ge(xw_ready, NB * KC)
                    pe.wait_ge(x1p_ready, (m + 1) * X1P)
                if (h, s) in LOGITS_STEP:
                    pe_logits(pe, m, LOGITS_STEP[h, s])
                if s < nup:
                    half_ups(pe, m, h, range(UPS[h][s - 1] if s else 0, UPS[h][s]))
                else:
                    r = HSTEPS[h] - nup
                    if s == nup:
                        pe.wait_ge(s2_in, (m * HALVES + h + 1) * 16)
                    downs(pe, m, h, lambda q, k: s2[:, q * PART + k * C:q * PART + (k + 1) * C], H_ORDER,
                          range((s - nup) * DOWNS // r, (s - nup + 1) * DOWNS // r), first_unit=(h == 0))

        def pe_expert(pe, m, e, step0, rnn=True):
            ups = JC * KC * len(THREE)
            for s in range(ESTEPS):
                if rnn:
                    pe_step(pe, step0 + s, s % 2)
                if s < UP_E:
                    expert_ups(pe, e, range(s * ups // UP_E, (s + 1) * ups // UP_E))
                else:
                    r = ESTEPS - UP_E
                    downs(pe, m, e + HALVES,
                          lambda q, k: we2[:, ds(e * (2 * PART) + (q * PART + k * C), C)], E_ORDER,
                          range((s - UP_E) * DOWNS // r, (s - UP_E + 1) * DOWNS // r))

        @block.tensor
        def _(pe):
            pe.wait_ge(consts, E + 4)
            pe_inputs(pe, 0, range(G))
            pe.wait_ge(small_in, 16 * (4 + B))
            for b in range(B):
                for k in range(KC):
                    last = nc.tensor.matmul(rbk[0:1, b * E:(b + 1) * E], ct[:, k, b, :], rw[:, KC + k, :],
                                            start=(k == 0), stop=(k == KC - 1))
            last.then_inc(t_ps, 1)
            pe.wait_ge(t_row, 1)
            for c in range(2):
                pe.wait_ge(w_split, c + 1)
                pe_xw(pe, 0, range(c * XW_ALL // 2, (c + 1) * XW_ALL // 2))
            pe.wait_ge(w_split, S0)
            pe.wait_ge(seeded, 2)
            def prepare(g):
                for s in range(XS):
                    pe_step(pe, g * XS + s, s % 2)
                    pe_ahead(pe, g, s)

            prepare(0)
            with pe.Fori(1, NB - 1) as g:
                prepare(g)
            prepare(NB - 1)
            pe.wait_ge(rw_split, 2)
            with pe.Fori(1, NB) as i:
                for h in range(HALVES):
                    pe_half(pe, i - 1, h, i * TB + H0[h])
                with pe.Fori(0, E) as e:
                    pe_expert(pe, i - 1, e, i * TB + e * ESTEPS + H0[HALVES])
            for h in range(HALVES):
                pe_half(pe, NB - 1, h, 0, rnn=False)
            with pe.Fori(0, E) as e:
                pe_expert(pe, NB - 1, e, 0, rnn=False)

        def act_step(act, n, t, par):
            act.wait_ge(pre_ready, n + 1)
            nc.scalar.activation(hp[:, :, 0, :, :], pre[:, :, :, :], ACT.Tanh, scale=1.0 / WS).then_inc(h_hi, 1)
            nc.scalar.activation(hist[:, :, :, ds(t, 1)], pre[:, :, :, :], ACT.Tanh, scale=1.0 / WS)\
              .then_inc(h_kept, 1)
            act_seed(xw[:, :, :, ds(t, 1)], par)

        def act_seed(src, par):
            nc.scalar.activation(z[par][:, :, 2, :], src.rearrange("p j b o -> p j (b o)"), ACT.Copy)\
              .then_inc(seeded, 1)

        def act_xt(act, i, c, dst):
            act.wait_ge(xt_ps, i * 2 + (c + 1))
            nc.scalar.activation(dst[:, 2 * c:2 * c + 2, :].rearrange("p k n -> p (k n)"), db[c][:, :], ACT.Copy)\
              .then_inc(xt_ready, 1)

        def act_xp(act, i, c, src):
            act.wait_ge(xt_ready, i * 2 + (c + 1))
            if not peeled(i, 0):
                if c == 0:
                    act.wait_ge(xp_used, i)
                else:
                    act.wait_ge(xw_ps, i * KC)
            nc.scalar.activation(xp[:, 0, 2 * c:2 * c + 2, :], src[:, 2 * c:2 * c + 2, :], ACT.Copy)\
              .then_inc(xp_hi, 1)

        def act_xw(act, i, j, t0, dst):
            act.wait_ge(xw_ps, i * KC + (j + 1))
            nc.scalar.activation(dst, ub[j][:, 0:N].rearrange("p (b t) -> p b t", b=B)[:, :, t0:],
                                 ACT.Identity, bias=b64[:, j:j + 1]).then_inc(xw_ready, 1)

        def act_out(act, i, j):
            if j == 0 and not peeled(i, 1):
                act.wait_ge(acc_free, (i - 1) * 16)
            act_xw(act, i, j, 0, acc[:, :, :].rearrange("p b c -> p (b c)")[:, j * N:(j + 1) * N]
                   .rearrange("p (b t) -> p b t", b=B))

        def act_ahead(act, g, s):
            if s == 0 and not peeled(g, 0, 1):
                act_out(act, g - 1, KC - 1)
            if s == 1 and not peeled(g, 0):
                act_xt_to_x1(act, g, 1)
            if s == 2 and not peeled(g, 0):
                act_xp(act, g, 1, x1)
            if s == 3 and not peeled(g, NB - 1):
                act_xt_to_x1(act, g + 1, 0)
            if s == 4 and not peeled(g, NB - 1):
                act_xp(act, g + 1, 0, x1)
            if s >= 5 and not peeled(g, 0):
                act_out(act, g, s - 5)

        def act_xt_to_x1(act, i, c):
            if not peeled(i, 1):
                act.wait_ge(xt_out[c], (i - 1) * 16)
                act.wait_ge(xp_ready, i * 2 + (c - 1))
            act_xt(act, i, c, x1)

        def act_x1p(act, m, c):
            g, t = x1_piece(c)
            act.wait_ge(x1_ready, m * PIECES + (PIECES if c == 2 else PIECES - 1))
            nc.scalar.activation(x1p[:, 0, :, :].rearrange("p k (b t) -> p (k b) t", b=B)[:, g, t],
                                 x1[:, :, :].rearrange("p k (b t) -> p (k b) t", b=B)[:, g, t], ACT.Copy)\
              .then_inc(x1_hi, 1)

        def act_acc(act, m, b):
            act.wait_ge(acc_free, (m + (NB - 1)) * 16)
            act.wait_ge(x1_rows, m * B + (b + 1))
            nc.scalar.activation(acc[:, b, :], db[b][:, :], ACT.Copy).then_inc(acc_set, 1)

        def act_gate(act, m, w, j, bank_no, func, scale):
            act.wait_ge(up_done, chunk_no(m, w, j) + 1)
            nc.scalar.activation(et[:, j % 2, :], ub[bank_no][:, 0:N], func, scale=scale).then_inc(act_done, 1)

        def act_hi(act, m, w, j, g, scale, done):
            act.wait_ge(done, (m * (HALVES * JC) + w * JC + j if done is g_done else chunk_no(m, w, j)) + 1)
            nc.scalar.activation(hid[:, j, 0, :], g[:, j % 2, :], ACT.Copy, scale=scale).then_inc(hid_hi, 1)

        H_GATE = [{5: 0, 7: 1, 10: 2, 12: 3}, {3: 0, 5: 1, 8: 2, 10: 3}]
        E_GATE = {2: 0, 3: 1, 5: 2, 6: 3}

        def act_half(act, m, h, step0, t0, rnn=True):
            if h == 0:
                act_x1p(act, m, 2)
            for s in range(HSTEPS[h]):
                if rnn:
                    act_step(act, step0 + s, t0 + s, (t0 + s) % 2)
                if (h, s) == (0, 4):
                    act.wait_ge(logits, (m + 1) * B)
                    nc.scalar.activation(nlog[:, :], rbk[:, 0:B * E], ACT.Copy, scale=-1.0 / WS)\
                      .then_inc(nlog_ready, 1)
                if (h, s) in ((0, 6), (0, 9)):
                    act_acc(act, m, (s - 6) // 3)
                if s in H_GATE[h]:
                    act_gate(act, m, h, H_GATE[h][s], 2 * (H_GATE[h][s] % 2), ACT.Tanh, 0.5 / WS)
                if s - 1 in H_GATE[h]:
                    act_hi(act, m, h, H_GATE[h][s - 1], gt, 1.0, g_done)

        def act_expert(act, m, e, step0, t0, rnn=True, last=False):
            for s in range(ESTEPS):
                if rnn:
                    act_step(act, step0 + s, t0 + s, s % 2)
                if s - 1 in E_GATE:
                    act_hi(act, m, e + HALVES, E_GATE[s - 1], et, GS, act_done)
                if s in E_GATE:
                    if E_GATE[s] >= 2:
                        act.wait_ge(hid_ready, chunk_no(m, e + HALVES, E_GATE[s] - 2) + 1)
                    act_gate(act, m, e + HALVES, E_GATE[s], E_GATE[s], ACT.Gelu, 1.0 / WS)
                if last and s in (7, 8):
                    act_x1p(act, m + 1, s - 7)

        def shared_part(g, q, k):
            place = we2[:, (2 + g) * 2 * PART:(3 + g) * 2 * PART]
            if g < 2 * HALVES:
                return place.rearrange("p (j q k c) -> p j q k c", j=JC, q=2, k=KC)[:, :, q, k, :]
            return place[:, q * PART + k * C:q * PART + (k + 1) * C]

        def shared_src(g, k):
            src = stage[:, g % 2, k * C:(k + 1) * C]
            return src.rearrange("p (j c) -> p j c", j=JC) if g < 2 * HALVES else src

        def split_hi(act, dst, src):
            nc.scalar.activation(dst, src, ACT.Copy, scale=WS).then_inc(w_hi, 1)

        @block.scalar
        def _(act):
            act.wait_ge(consts, E + 4)
            nc.scalar.activation(hp[:, 0, 0, :, 0], ident[:, 0:B], ACT.Gelu).then_inc(table_set, 1)
            for c in range(2):
                act_xt(act, 0, c, xt)
            for c in range(2):
                act_xp(act, 0, c, xt)
            act.wait_ge(small_in, 16 * (4 + B))
            act.wait_ge(table_set, 1)
            nc.scalar.activation(hp[:, :, 0, :, :], ct[:, :, :, :], ACT.Copy).then_inc(h_hi, 1)
            act.wait_ge(t_ps, 1)
            nc.scalar.activation(trow[0:1, :], rbk[0:1, 0:B * E], ACT.Copy, scale=WS).then_inc(t_row, 1)
            act.wait_ge(t_row, 1)
            nc.scalar.activation(trp[0:1, 0, :], trow[0:1, :], ACT.Copy).then_inc(rw_hi, 1)
            nc.scalar.activation(rwp[:, 0, :, :], rw[:, 0:KC, :], ACT.Copy, scale=WS).then_inc(rw_hi, 1)
            for n in range(S0):
                g, c = n // 2, n % 2
                act.wait_ge(wxh_in[n], 16)
                nc.scalar.activation(w0_slice((wx, wh)[g], c), w0_slice(stage[:, g, :], c), ACT.Copy, scale=WS)\
                  .then_inc(w_hi, 1)
            act.wait_ge(b_scaled, 1)
            for j in range(KC):
                act.wait_ge(xw_ps, j + 1)
                nc.scalar.activation(xw0[:, j, :, :], ub[j][:, 0:N].rearrange("p (b t) -> p b t", b=B)[:, :, 0:2],
                                     ACT.Identity, bias=b64[:, j:j + 1]).then_inc(xw0_ready, 1)
                act_xw(act, 0, j, 2, xw[:, j, :, 0:TB - 2])
            act.wait_ge(xw0_ready, KC)
            for t in range(2):
                act_seed(xw0[:, :, :, t:t + 1], t)
            act.wait_ge(xw_ready, KC)
            for g in range(NSH // 2):
                for s in range(XS):
                    act_step(act, g * XS + s, g * XS + s, s % 2)
                    for c, c0, n in (SPLIT_SHARED[s] if s < XS - 1 else ()):
                        if c0 == 0:
                            act.wait_ge(staged[c], 16 * (g + 1))
                        split_hi(act, shared_part(2 * g + c, 0, c0 // C), shared_src(2 * g + c, c0 // C))
                    act_ahead(act, g, s)

            def experts(e0, e1, left=None):
                with act.Fori(e0, e1) as e:
                    for s in range(XS):
                        t = e * XS + (NSH // 2 * XS + s)
                        act_step(act, t, t, s % 2)
                        for c, c0, n in (SPLIT_EXPERT[s] if s < XS - 1 else ()):
                            if c0 == 0:
                                act.wait_ge(staged[c], e * 16 + 16 * (NSH // 2 + 1))
                                if left is not None and c == 1:
                                    act.wait_ge(*left)
                            split_hi(act, (we1, we2)[c][:, ds(e * (2 * PART) + c0, n)], stage[:, c, c0:c0 + n])
                        act_ahead(act, e + NSH // 2, s)

            experts(0, 2)
            experts(2, 2 + 2 * HALVES, (scratch_out[0], 16 * 2 * HALVES))
            experts(2 + 2 * HALVES, E, (scratch_out[1], 16 * HALVES))
            with act.Fori(NSH // 2 + E, NB - 1) as g:
                for s in range(XS):
                    act_step(act, g * XS + s, g * XS + s, s % 2)
                    act_ahead(act, g, s)
            act.wait_ge(tail_in, 16)
            for s in range(XS):
                t = (NB - 1) * XS + s
                act_step(act, t, t, t % 2)
                act_ahead(act, NB - 1, s)
                if s in (5, 6):
                    act_x1p(act, 0, s - 5)
            act_out(act, NB - 1, KC - 1)
            with act.Fori(1, NB) as i:
                act.wait_ge(xw_in[0], i * 16)
                for h in range(HALVES):
                    act_half(act, i - 1, h, i * TB + H0[h], H0[h])
                act.wait_ge(xw_in[1], i * 16)
                with act.Fori(0, E - 1) as e:
                    act_expert(act, i - 1, e, i * TB + e * ESTEPS + H0[HALVES], e * ESTEPS + H0[HALVES])
                act_expert(act, i - 1, E - 1, i * TB + TC, TC, last=True)
            for h in range(HALVES):
                act_half(act, NB - 1, h, 0, 0, rnn=False)
            with act.Fori(0, E) as e:
                act_expert(act, NB - 1, e, 0, 0, rnn=False)

        def dve_step(dve, n, t, par):
            dve.wait_ge(z_ready, n + 1)
            nc.vector.tensor_reduce(pre[:, :, :, 0], z[par].rearrange("p j c b -> p j b c"), axis=AX.X, op=ALU.add)\
              .then_inc(pre_ready, 1)
            dve.wait_ge(h_hi, n + 2)
            dve.wait_ge(h_kept, n + 1)
            nc.vector.tensor_tensor(hp[:, :, 1, :, :], hist[:, :, :, ds(t, 1)], hp[:, :, 0, :, :], ALU.subtract)\
              .then_inc(h_ready, 1)

        GATE_AT = (0, 5, 9, 13, 17, 22, 26)
        CHAIN = GATE_AT[-1]

        GATE_STEP = {(0, 9): 0, (0, 14): 1, (0, 15): 2, (1, 1): 3, (1, 2): 4, (1, 7): 5}

        def dve_gates(dve, m, stage_no):
            count = [GATE_AT[stage_no]]

            def link(ins):
                count[0] += 1
                ins.then_inc(chain, 1)
                dve.wait_ge(chain, m * CHAIN + count[0])

            def is_max():
                link(nc.vector.tensor_reduce(mx[:, :, 0], sel[:, :, :], axis=AX.X, op=ALU.max))
                link(nc.vector.tensor_tensor(m1[:, :, :], sel[:, :, :], mx[:, :, :].to_broadcast([P, B, E]),
                                             ALU.is_ge))

            def lowest(onehot):
                link(nc.vector.tensor_tensor(m1[:, :, :], m1[:, :, :], rev[:, :, :], ALU.mult))
                link(nc.vector.tensor_reduce(mx[:, :, 0], m1[:, :, :], axis=AX.X, op=ALU.max))
                link(nc.vector.tensor_tensor(onehot[:, :, :], m1[:, :, :], mx[:, :, :].to_broadcast([P, B, E]),
                                             ALU.is_equal))

            if stage_no == 0:
                dve.wait_ge(pow_ready, m + 1)
                link(nc.vector.tensor_scalar(pw[:, :], pw[:, :], 1.0, None, ALU.add))
                link(nc.vector.reciprocal(sg[:, :, :].rearrange("p b e -> p (b e)"), pw[:, :]))
                link(nc.vector.tensor_tensor(sel[:, :, :], sg[:, :, :], rb[:, :, :], ALU.add))
                is_max()
            if stage_no == 1:
                lowest(oh1)
                link(nc.vector.scalar_tensor_tensor(out=sel[:, :, :], in0=oh1[:, :, :], scalar=-BIG,
                                                    in1=sel[:, :, :], op0=ALU.mult, op1=ALU.add))
            if stage_no == 2:
                is_max()
                link(nc.vector.tensor_tensor(m1[:, :, :], m1[:, :, :], rev[:, :, :], ALU.mult))
                link(nc.vector.tensor_reduce(mx[:, :, 0], m1[:, :, :], axis=AX.X, op=ALU.max))
            if stage_no == 3:
                link(nc.vector.tensor_tensor(oh2[:, :, :], m1[:, :, :], mx[:, :, :].to_broadcast([P, B, E]),
                                             ALU.is_equal))
                link(nc.vector.tensor_tensor(m1[:, :, :], oh1[:, :, :], oh2[:, :, :], ALU.add))
                link(nc.vector.tensor_tensor(oh1[:, :, :], m1[:, :, :], sg[:, :, :], ALU.mult))
                link(nc.vector.tensor_reduce(den[:, :, 0], oh1[:, :, :], axis=AX.X, op=ALU.add))
            if stage_no == 4:
                link(nc.vector.tensor_scalar(okd[:, :, :], den[:, :, :], 1e-9, OS, ALU.is_gt, ALU.mult))
                link(nc.vector.tensor_scalar(alt[:, :, :], okd[:, :, :], -0.5, 0.5 * OS, ALU.mult, ALU.add))
                link(nc.vector.tensor_scalar(den[:, :, :], den[:, :, :], 1e-9, None, ALU.add))
                link(nc.vector.reciprocal(den[:, :, :], den[:, :, :]))
                link(nc.vector.tensor_tensor(den[:, :, :], den[:, :, :], okd[:, :, :], ALU.mult))
            if stage_no == 5:
                for b in range(B):
                    link(nc.vector.tensor_scalar(oh2[:, b, :], m1[:, b, :], alt[:, b, :], None, ALU.mult))
                for b in range(B):
                    link(nc.vector.scalar_tensor_tensor(out=gates[:, b * (1 + E) + 1:(b + 1) * (1 + E)],
                                                        in0=oh1[:, b, :],
                                                        scalar=den[:, b, :], in1=oh2[:, b, :],
                                                        op0=ALU.mult, op1=ALU.add))
            assert count[0] == GATE_AT[stage_no + 1]

        def dve_silu(dve, m, h, j):
            a, b = ub[2 * (j % 2)][:, 0:N], ub[2 * (j % 2) + 1][:, 0:N]
            dve.wait_ge(act_done, chunk_no(m, h, j) + 1)
            nc.vector.scalar_tensor_tensor(out=ut[:, :], in0=et[:, j % 2, :], scalar=1.0, in1=a,
                                           op0=ALU.add, op1=ALU.mult).then_inc(u_done, 1)
            dve.wait_ge(u_done, m * (HALVES * JC) + (h * JC + j + 1))
            nc.vector.scalar_tensor_tensor(out=gt[:, j % 2, :], in0=ut[:, :], scalar=GS / (2.0 * WS * WS), in1=b,
                                           op0=ALU.mult, op1=ALU.mult).then_inc(g_done, 1)

        def dve_lo(dve, m, w, j, g, scale):
            dve.wait_ge(hid_hi, chunk_no(m, w, j) + 1)
            nc.vector.scalar_tensor_tensor(out=hid[:, j, 1, :], in0=g[:, j % 2, :], scalar=scale,
                                           in1=hid[:, j, 0, :], op0=ALU.mult, op1=ALU.subtract)\
               .then_inc(hid_ready, 1)

        def dve_add(dve, m, w, b, scalar):
            dve.wait_ge(added, unit_no(m, w) * B + (b + 1))
            dve.wait_ge(down_done, unit_no(m, w) * B + (b + 1))
            nc.vector.scalar_tensor_tensor(out=acc[:, b, :], in0=db[b][:, :], scalar=scalar, in1=acc[:, b, :],
                                           op0=ALU.mult, op1=ALU.add).then_inc(added, 1)

        def dve_half(dve, m, h, step0, t0, rnn=True):
            for s in range(HSTEPS[h]):
                if rnn:
                    dve_step(dve, step0 + s, t0 + s, (t0 + s) % 2)
                if (h, s) in GATE_STEP:
                    dve_gates(dve, m, GATE_STEP[h, s])
                if s in H_GATE[h]:
                    dve_silu(dve, m, h, H_GATE[h][s])
                if s - 1 in H_GATE[h]:
                    dve_lo(dve, m, h, H_GATE[h][s - 1], gt, 1.0)
                if s == HSTEPS[h] - 1:
                    if h == 0:
                        dve.wait_ge(acc_set, (m + 1) * B)
                    dve_add(dve, m, h, 0, OS)
                if s == 0 and h > 0:
                    dve_add(dve, m, h - 1, 1, OS)

        def dve_expert(dve, m, e, step0, t0, rnn=True):
            for s in range(ESTEPS):
                if rnn:
                    dve_step(dve, step0 + s, t0 + s, s % 2)
                if s - 1 in E_GATE:
                    dve_lo(dve, m, e + HALVES, E_GATE[s - 1], et, GS)
                if s == 0:
                    dve_add(dve, m, e + (HALVES - 1), 1, gates[:, ds(e + (1 + E), 1)])
                if s == UP_E + 3:
                    dve_add(dve, m, e + HALVES, 0, gates[:, ds(e + 1, 1)])

        def split_lo(dve, count, dst, hi, src):
            dve.wait_ge(w_hi, count)
            nc.vector.scalar_tensor_tensor(out=dst, in0=src, scalar=WS, in1=hi, op0=ALU.mult, op1=ALU.subtract)\
              .then_inc(w_split, 1)

        @block.vector
        def _(dve):
            dve.wait_ge(consts, E + 4)
            dve.wait_ge(small_in, 16 * (4 + B))
            nc.vector.tensor_scalar(b64[:, :], b64[:, :], WS, None, ALU.mult).then_inc(b_scaled, 1)
            nc.vector.memset(gates[:, :], OS).then_inc(added, 1)
            dve.wait_ge(h_hi, 1)
            nc.vector.tensor_tensor(hp[:, :, 1, :, :], ct[:, :, :, :], hp[:, :, 0, :, :], ALU.subtract)\
              .then_inc(h_ready, 1)
            dve.wait_ge(rw_hi, 1)
            nc.vector.tensor_tensor(trp[0:1, 1, :], trow[0:1, :], trp[0:1, 0, :], ALU.subtract).then_inc(rw_split, 1)
            dve.wait_ge(rw_hi, 2)
            nc.vector.scalar_tensor_tensor(out=rwp[:, 1, :, :], in0=rw[:, 0:KC, :], scalar=WS, in1=rwp[:, 0, :, :],
                                           op0=ALU.mult, op1=ALU.subtract).then_inc(rw_split, 1)
            for n in range(S0):
                g, c = n // 2, n % 2
                w = (wx, wh)[g]
                split_lo(dve, n + 1, w0_slice(w, c, 1), w0_slice(w, c), w0_slice(stage[:, g, :], c))
            for g in range(NSH // 2):
                done = S0 + g * 2 * SL
                for s in range(XS):
                    dve_step(dve, g * XS + s, g * XS + s, s % 2)
                    for c, c0, n in (SPLIT_SHARED[s - 1] if s > 0 else ()):
                        done += 1
                        split_lo(dve, done, shared_part(2 * g + c, 1, c0 // C), shared_part(2 * g + c, 0, c0 // C),
                                 shared_src(2 * g + c, c0 // C))
            with dve.Fori(0, E) as e:
                done = S0 + NSH * SL
                for s in range(XS):
                    t = e * XS + (NSH // 2 * XS + s)
                    dve_step(dve, t, t, s % 2)
                    for c, c0, n in (SPLIT_EXPERT[s - 1] if s > 0 else ()):
                        done += 1
                        w = (we1, we2)[c]
                        split_lo(dve, e * SE + done, w[:, ds(e * (2 * PART) + (PART + c0), n)],
                                 w[:, ds(e * (2 * PART) + c0, n)], stage[:, c, c0:c0 + n])
            with dve.Fori(NSH // 2 + E, NB) as g:
                for s in range(XS):
                    dve_step(dve, g * XS + s, g * XS + s, s % 2)
            with dve.Fori(1, NB) as i:
                for h in range(HALVES):
                    dve_half(dve, i - 1, h, i * TB + H0[h], H0[h])
                with dve.Fori(0, E) as e:
                    dve_expert(dve, i - 1, e, i * TB + e * ESTEPS + H0[HALVES],
                               e * ESTEPS + H0[HALVES])
                dve_add(dve, i - 1, UNITS - 1, 1, gates[:, B * (1 + E) - 1:B * (1 + E)])
            for h in range(HALVES):
                dve_half(dve, NB - 1, h, 0, 0, rnn=False)
            with dve.Fori(0, E) as e:
                dve_expert(dve, NB - 1, e, 0, 0, rnn=False)
            dve_add(dve, NB - 1, UNITS - 1, 1, gates[:, B * (1 + E) - 1:B * (1 + E)])


_INS = ["x", "cond_1024", "L0_cond_Wx", "L0_cond_Wh", "L0_cond_b", "L1_cond_router_W", "L1_cond_router_bias",
        "L1_cond_w1", "L1_cond_w3", "L1_cond_w2", "L1_cond_W1e", "L1_cond_W2e"]


def kernel(**inputs):
    import numpy as _np
    import concourse.bacc as _bacc
    from concourse import mybir as _mybir
    from concourse.bass_utils import run_bass_kernel_spmd as _run

    nc = _bacc.Bacc("TRN2", target_bir_lowering=False, num_devices=1)
    arrays, args = {}, []
    for name in _INS:
        a = _np.ascontiguousarray(inputs[name])
        arrays[f"in_{name}"] = a
        args.append(nc.dram_tensor(f"in_{name}", a.shape, _mybir.dt.from_np(a.dtype), kind="ExternalInput").ap())
    shape = inputs["x"].shape
    args.append(nc.dram_tensor("out_0", shape, _mybir.dt.float32, kind="ExternalOutput").ap())
    rnn_then_moe_kernel(nc, *args)
    r = _run(nc, [arrays], core_ids=[0])
    return r.results[0]["out_0"]
```
